# Optimizing a Trainium2 kernel written in Bass

```python
import numpy as np
import jax
import jax.numpy as jnp

def _softmax(x, axis=-1):
    return jax.nn.softmax(x, axis=axis)

def _gelu(x):
    return jax.nn.gelu(x, approximate=True)

def _silu(x):
    return jax.nn.silu(x)

def _sigmoid(x):
    return jax.nn.sigmoid(x)

def _layernorm(x, axis=-1, eps=1e-05):
    m = jnp.mean(x, axis=axis, keepdims=True)
    v = jnp.var(x, axis=axis, keepdims=True)
    return (x - m) / jnp.sqrt(v + eps)

def _scatter_add(tgt, idx, src, axis=0):
    return tgt.at[idx].add(src)

def _segment_sum(src, seg, n):
    return jax.ops.segment_sum(src, seg, n)
kernel_name = 'mk_gnn_resnorm_d1_gnn_r64_1c26e5'

def setup_inputs(seed: int=0):
    np.random.seed(seed)
    _w = jnp.asarray

    def _rec_inputs():
        import jax
        import jax.numpy as jnp
        _gk = jax.random.key(seed)
        x = -0.0005121 + 1.001 * jax.random.normal(jax.random.fold_in(_gk, 1), (50000, 64), jnp.float32)
        src = jax.random.randint(jax.random.fold_in(_gk, 2), (25000,), 0, 50000, jnp.int32)
        dst = jax.random.randint(jax.random.fold_in(_gk, 3), (25000,), 0, 50000, jnp.int32)
        _o = jnp.argsort(dst, stable=True)
        src = src[_o]
        dst = dst[_o]
        edge_attr_64 = -9.77346e-05 + 0.999888 * jax.random.normal(jax.random.fold_in(_gk, 12), (25000, 64), jnp.float32)
        return (x, src, dst, edge_attr_64)
    x, src, dst, edge_attr_64 = _rec_inputs()

    def _L0_gnn_setup():
        import jax, jax.numpy as jnp
        import numpy as np
        N_NODES = 50000
        key = jax.random.key(seed)
        ks = jax.random.split(key, 8)
        d = 64
        n_edges = 12500
        h = 256
        in_dim = 3 * d
        return {'node_feat': jax.random.normal(ks[0], (N_NODES, d), dtype=jnp.float32), 'edge_feat': jax.random.normal(ks[1], (n_edges, d), dtype=jnp.float32), 'senders': jax.random.randint(ks[2], (n_edges,), 0, N_NODES, dtype=jnp.int32), 'receivers': jax.random.randint(ks[3], (n_edges,), 0, N_NODES, dtype=jnp.int32), 'W1': jax.random.normal(ks[4], (in_dim, h), dtype=jnp.float32) * (1.0 / np.sqrt(in_dim)), 'b1': jnp.zeros((h,), dtype=jnp.float32), 'W2': jax.random.normal(ks[5], (h, d), dtype=jnp.float32) * (1.0 / np.sqrt(h)), 'b2': jnp.zeros((d,), dtype=jnp.float32)}
    _L0_gnn_all = _L0_gnn_setup()
    _L0_gnn_in = {k: v for k, v in _L0_gnn_all.items() if k in ('W1', 'b1', 'W2', 'b2')}
    del _L0_gnn_all
    return {'x': x, 'src': src, 'dst': dst, 'edge_attr_64': edge_attr_64, 'L0_gnn_W1': _L0_gnn_in['W1'], 'L0_gnn_b1': _L0_gnn_in['b1'], 'L0_gnn_W2': _L0_gnn_in['W2'], 'L0_gnn_b2': _L0_gnn_in['b2']}

def reference(x, src, dst, edge_attr_64, L0_gnn_W1, L0_gnn_b1, L0_gnn_W2, L0_gnn_b2):
    import jax
    import jax.numpy as jnp

    def _L0_gnn_ref(node_feat, edge_feat, senders, receivers, W1, b1, W2, b2):
        import jax, jax.numpy as jnp
        import numpy as np
        N_NODES = 50000
        in_agg = jax.ops.segment_sum(edge_feat, receivers, num_segments=N_NODES)
        out_agg = jax.ops.segment_sum(edge_feat, senders, num_segments=N_NODES)
        upd_in = jnp.concatenate([in_agg, out_agg, node_feat], axis=1)
        hcat = jax.nn.relu(upd_in @ W1 + b1)
        return hcat @ W2 + b2
    x = _layernorm(x + _L0_gnn_ref(x, edge_attr_64, src, dst, L0_gnn_W1, L0_gnn_b1, L0_gnn_W2, L0_gnn_b2), axis=-1)
    return x

_drawn_inputs = setup_inputs


def setup_inputs(seed=0):
    import zlib

    import numpy as np

    out = dict(_drawn_inputs(seed))
    spreads = {'L0_gnn_b1': (0.0, 0.1), 'L0_gnn_b2': (0.0, 0.1)}
    factors = {}
    for name, (base, spread) in spreads.items():
        noise = np.random.default_rng([zlib.crc32(name.encode()), seed]).standard_normal(out[name].shape)
        drawn = base * np.exp(spread * noise) if base else spread * noise
        out[name] = jnp.asarray(drawn.astype(out[name].dtype))
    for name, factor in factors.items():
        out[name] = (out[name] * factor).astype(out[name].dtype)
    return out
```

```python
import concourse.bass as bass
from concourse import mybir
from contextlib import ExitStack

ALU = mybir.AluOpType
ACT = mybir.ActivationFunctionType
F32 = mybir.dt.float32
I32 = mybir.dt.int32
AX_X = mybir.AxisListType.X

P = 128
D = 64
H = 256
N_NODES = 50000
N_EDGES = 25000
MACRO = 4 * P
MACROS = 98
N_PAD = MACROS * MACRO
BINS = N_PAD // P
ET = -(-N_EDGES // P)
E_PAD = ET * P
ROW = D + 2
TRASH = N_PAD
EPS = 1e-5


def gnn_kernel(nc, x, src, dst, edge, w1, b1, w2, b2, out):
    in_rows = nc.dram_tensor("in_rows", [N_PAD + P, ROW], F32)
    out_rows = nc.dram_tensor("out_rows", [N_PAD + P, ROW], F32)
    tables = [out_rows, in_rows]
    with ExitStack() as ctx:
        def sb(name, shape, dt=F32):
            return ctx.enter_context(nc.sbuf_tensor(name, shape, dt))

        def psum(name, shape, dt=F32):
            return ctx.enter_context(nc.psum_tensor(name, shape, dt))

        def sem(name):
            return ctx.enter_context(nc.semaphore(name))

        ident = sb("ident", [P, P])
        earlier = sb("earlier", [P, P])
        iota_row = sb("iota_row", [P, P])
        w_agg = sb("w_agg", [P, H])
        w_x = sb("w_x", [P, H])
        w_2 = sb("w_2", [P, 2, D])
        b_1 = sb("b_1", [P, 2])
        b_2 = sb("b_2", [P, D])
        eps = sb("eps", [P, 1])
        edges = sb("edges", [P, ET, D])
        ends_i = sb("ends_i", [P, 2, ET], I32)
        ends = sb("ends", [P, 2, ET])
        window_start = sb("window_start", [1, BINS], I32)
        init = sb("init", [P, BINS // 4, ROW])
        trash_row = sb("trash_row", [P, 1])
        idx_wide = [sb(f"idx_wide{j}", [P, P]) for j in range(2)]
        same = [sb(f"same{j}", [P, P]) for j in range(2)]
        junk = sb("junk", [P, P])
        dup = [sb(f"dup{j}", [P, 4]) for j in range(2)]
        row_index = [sb(f"row_index{j}", [P, 1], I32) for j in range(2)]
        stage = [sb(f"stage{j}", [P, ROW]) for j in range(2)]
        x_t = [sb(f"x_t{b}", [P, 4, D]) for b in range(2)]
        rows_t = [[sb(f"rows_t{j}{b}", [P, 4, ROW]) for b in range(2)] for j in range(2)]
        base = sb("base", [P, 4])
        in_local = [sb(f"in_local{b}", [P, 4]) for b in range(2)]
        hot = [[sb(f"hot{j}{b}", [P, 4, P]) for b in range(2)] for j in range(2)]
        agg_T = [sb(f"agg_T{b}", [P, MACRO]) for b in range(2)]
        x_T = [sb(f"x_T{b}", [P, 2, P]) for b in range(2)]
        hid = [sb(f"hid{b}", [P, 2, MACRO]) for b in range(2)]
        xb = [sb(f"xb{b}", [P, 4, D]) for b in range(2)]
        res = [sb(f"res{b}", [P, 4, D]) for b in range(2)]
        stats = [sb(f"stats{b}", [P, 4, 6]) for b in range(2)]
        both = [sb(f"both{b}", [P, 4, 2]) for b in range(2)]
        apart = [sb(f"apart{b}", [P, 4]) for b in range(2)]
        apart_sq = [sb(f"apart_sq{b}", [P, 4]) for b in range(2)]
        mean = [sb(f"mean{b}", [P, 4]) for b in range(2)]
        var_d = [sb(f"var_d{b}", [P, 4]) for b in range(2)]
        std = [sb(f"std{b}", [P, 4]) for b in range(2)]
        rstd = [sb(f"rstd{b}", [P, 4]) for b in range(2)]
        y_t = [sb(f"y_t{b}", [P, 4, D]) for b in range(2)]

        ps_agg = psum("ps_agg", [P, MACRO])
        ps_x = psum("ps_x", [P, 4, P])
        ps_hid = [psum(f"ps_hid{b}", [P, 2, MACRO]) for b in range(2)]
        ps_y = [psum(f"ps_y{b}", [P, 4, P]) for b in range(2)]

        weights_in = sem("weights_in")
        edges_in = sem("edges_in")
        consts = sem("consts")
        init_made = sem("init_made")
        table_settled = [sem("out_settled"), sem("in_settled")]
        ends_ready = sem("ends_ready")
        idx_wide_ready = [sem(f"idx_wide_ready{j}") for j in range(2)]
        idx_row_ready = [sem(f"idx_row_ready{j}") for j in range(2)]
        same_ready = [sem(f"same_ready{j}") for j in range(2)]
        dup_chain = [sem(f"dup_chain{j}") for j in range(2)]
        additions_begun = sem("additions_begun")
        sums_ready = [sem(f"sums_ready{j}") for j in range(2)]
        stage_ready = [sem(f"stage_ready{j}") for j in range(2)]
        x_in = [sem(f"x_in{b}") for b in range(2)]
        rows_in = [sem(f"rows_in{b}") for b in range(2)]
        local_ready = sem("local_ready")
        hot_ready = sem("hot_ready")
        agg_ready = sem("agg_ready")
        xT_ready = sem("xT_ready")
        agg_copied = sem("agg_copied")
        xT_copied = sem("xT_copied")
        hid_crossed = sem("hid_crossed")
        hid_ready = sem("hid_ready")
        relu_done = sem("relu_done")
        y_ready = sem("y_ready")
        xb_ready = sem("xb_ready")
        res_ready = sem("res_ready")
        stats_ready = sem("stats_ready")
        mv_chain = sem("mv_chain")
        mv_ready = sem("mv_ready")
        std_ready = sem("std_ready")
        rstd_ready = sem("rstd_ready")
        y_done = sem("y_done")
        stored = [sem(f"stored{b}") for b in range(2)]

        INIT = 5 * 16
        HALF = MACROS // 2

        block = ctx.enter_context(nc.Block())

        @block.sync
        def _(sp):
            for k, e in enumerate((src, dst)):
                sp.dma_start(ends_i[:, k, :], e.rearrange("(p t) -> p t", p=P)).then_inc(edges_in, 16)
            sp.dma_start(edges[:], edge.rearrange("(p t) d -> p t d", p=P)).then_inc(edges_in, 16)
            sp.dma_start(w_agg[:], w1[0:P, :]).then_inc(weights_in, 16)
            for half in range(2):
                sp.dma_start(w_x[half * D:(half + 1) * D, :], w1[P:P + D, :]).then_inc(weights_in, 16)
            sp.dma_start(w_2[:], w2.rearrange("(c p) d -> p c d", p=P)).then_inc(weights_in, 16)
            with nc.allow_non_contiguous_dma(reason="256 values"):
                sp.dma_start(b_1[:], b1.rearrange("(c p) -> p c", p=P)).then_inc(weights_in, 16)
            sp.dma_start(b_2[:], b2.rearrange("(o d) -> o d", o=1).to_broadcast([P, D])).then_inc(weights_in, 16)

            for j in range(2):
                sp.wait_ge(table_settled[j], INIT + 16 * ET)

            def load(k, b, first=False):
                m = k * 2 + b
                if not first:
                    sp.wait_ge(agg_ready, m - 1)
                    sp.wait_ge(hot_ready, m - 1)
                    sp.wait_ge(xb_ready, m - 1)
                sp.dma_start(x_t[b][:], x[bass.ds(m * MACRO, MACRO), :].rearrange("(j p) d -> p j d", p=P)).then_inc(x_in[b], 16)
                sp.dma_start(rows_t[0][b][:], out_rows[bass.ds(m * MACRO, MACRO), :].rearrange("(j p) d -> p j d", p=P)).then_inc(rows_in[b], 16)
                for j in range(4):
                    s = sp.value_load(window_start[0:1, bass.ds(m * 4 + j, 1)], min_val=0, max_val=N_PAD - P)
                    sp.dma_start(rows_t[1][b][:, j, :], in_rows[bass.ds(s, P), :]).then_inc(rows_in[b], 16)

            load(0, 0, True)
            load(0, 1, True)
            with sp.Fori(1, HALF) as k:
                load(k, 0)
                load(k, 1)

        @block.gpsimd
        def _(pool):
            nc.gpsimd.memset(ident[:], 0.0).then_inc(init_made, 1)
            nc.gpsimd.memset(earlier[:], 1.0).then_inc(init_made, 1)
            nc.gpsimd.memset(eps[:], EPS).then_inc(consts, 1)
            nc.gpsimd.memset(init[:], 0.0).then_inc(init_made, 1)
            nc.gpsimd.memset(stage[0][:], 0.0).then_inc(consts, 1)
            nc.gpsimd.memset(stage[1][:], 0.0).then_inc(consts, 1)
            nc.gpsimd.iota(iota_row[:], [[1, P]], base=0, channel_multiplier=0, allow_small_or_imprecise_dtypes=True).then_inc(consts, 1)
            nc.gpsimd.iota(base[:], [[P, 4]], base=0, channel_multiplier=0, allow_small_or_imprecise_dtypes=True).then_inc(consts, 1)
            nc.gpsimd.iota(trash_row[:], [[0, 1]], base=TRASH, channel_multiplier=1, allow_small_or_imprecise_dtypes=True).then_inc(consts, 1)
            nc.gpsimd.iota(window_start[:], [[P, BINS]], base=0, channel_multiplier=0).then_inc(consts, 1)
            pool.wait_ge(init_made, 3)
            nc.gpsimd.affine_select(out=ident[:], in_=ident[:], compare_op=ALU.not_equal, fill=1.0, base=0, pattern=[[-1, P]], channel_multiplier=1).then_inc(consts, 1)
            nc.gpsimd.affine_select(out=earlier[:], in_=earlier[:], compare_op=ALU.is_gt, fill=0.0, base=0, pattern=[[-1, P]], channel_multiplier=1).then_inc(consts, 1)
            nc.gpsimd.iota(init[:, :, D:D + 1], [[0, BINS // 4]], base=0, channel_multiplier=1, allow_small_or_imprecise_dtypes=True).then_inc(init_made, 1)
            for q in range(4):
                lo = q * (BINS // 4) * P
                if q:
                    for j in range(2):
                        pool.wait_ge(table_settled[j], 16 * q)
                nc.gpsimd.iota(init[:, :, D + 1:D + 2], [[P, BINS // 4]], base=lo, channel_multiplier=1, allow_small_or_imprecise_dtypes=True).then_inc(init_made, 1)
                pool.wait_ge(init_made, 5 + q)
                for j in range(2):
                    pool.dma_start(tables[j][lo:lo + (BINS // 4) * P, :].rearrange("(c p) d -> p c d", p=P), init[:]).then_inc(table_settled[j], 16)
            for j in range(2):
                pool.dma_start(tables[j][TRASH:TRASH + P, :], init[:, 0, :]).then_inc(table_settled[j], 16)
            with pool.Fori(0, ET) as t:
                for j in range(2):
                    pool.wait_ge(stage_ready[j], t + 1)
                    pool.wait_ge(dup_chain[j], t * 4 + 4)
                    pool.wait_ge(table_settled[j], t * 16 + INIT)
                    pool.sem_inc(additions_begun, 1)
                    nc.gpsimd.indirect_dma_start(
                        out=tables[j][:, :], out_offset=bass.IndirectOffsetOnAxis(ap=row_index[j][:], axis=0),
                        in_=stage[j][:], in_offset=None, compute_op=ALU.add).then_inc(table_settled[j], 16)

            pool.wait_ge(weights_in, 6 * 16)

            def step(k, b, first=False):
                m = k * 2 + b
                pool.wait_ge(x_in[b], k * 16 + 16)
                if not first:
                    pool.wait_ge(res_ready, m - 1)
                nc.gpsimd.tensor_tensor(xb[b][:], x_t[b][:], b_2[:].unsqueeze(1).to_broadcast([P, 4, D]), ALU.add).then_inc(xb_ready, 1)

            def store(k, b):
                m = k * 2 + b
                pool.wait_ge(y_done, m + 1)
                pool.dma_start(out[bass.ds(m * MACRO, MACRO), :].rearrange("(j p) d -> p j d", p=P), y_t[b][:]).then_inc(stored[b], 16)

            step(0, 0, True)
            step(0, 1, True)
            with pool.Fori(1, HALF) as k:
                for b in range(2):
                    step(k, b)
                    store(k - 1, b)
            for b in range(2):
                store(HALF - 1, b)
            for b in range(2):
                pool.wait_ge(stored[b], 16 * HALF)

        @block.vector
        def _(dve):
            dve.wait_ge(edges_in, 3 * 16)
            nc.vector.tensor_copy(ends[:], ends_i[:]).then_inc(ends_ready, 1)
            dve.wait_ge(ends_ready, 1)
            dve.wait_ge(consts, 9)
            with dve.Fori(0, ET) as t:
                for j in range(2):
                    nc.vector.tensor_copy(idx_wide[j][:], ends[:, j, bass.ds(t, 1)].to_broadcast([P, P])).then_inc(idx_wide_ready[j], 1)
                for j in range(2):
                    dve.wait_ge(idx_row_ready[j], t + 1)
                    nc.vector.tensor_scalar(same[j][:], ps_hid[j][:, 0, 0:P], idx_wide[j][:, 0:1], None, ALU.is_equal).then_inc(same_ready[j], 1)
                    dve.wait_ge(same_ready[j], t + 1)
                    nc.vector.tensor_tensor_reduce(out=junk[:], in0=same[j][:], in1=earlier[:], scale=1.0, scalar=0.0, op0=ALU.mult, op1=ALU.add, accum_out=dup[j][:, 0:1]).then_inc(dup_chain[j], 1)
                    nc.vector.tensor_tensor(dup[j][:, 1:2], trash_row[:], idx_wide[j][:, 0:1], ALU.subtract).then_inc(dup_chain[j], 1)
                    dve.wait_ge(dup_chain[j], t * 4 + 2)
                    nc.vector.tensor_scalar(dup[j][:, 2:3], dup[j][:, 0:1], 1.0, dup[j][:, 1:2], ALU.min, ALU.mult).then_inc(dup_chain[j], 1)
                    dve.wait_ge(dup_chain[j], t * 4 + 3)
                    dve.wait_ge(table_settled[j], t * 16 + INIT)
                    nc.vector.tensor_tensor(row_index[j][:], dup[j][:, 2:3], idx_wide[j][:, 0:1], ALU.add).then_inc(dup_chain[j], 1)
                    dve.wait_ge(dup_chain[j], t * 4 + 4)

            def hots(k, b, first=False):
                m = k * 2 + b
                dve.wait_ge(rows_in[b], k * 80 + 80)
                nc.vector.tensor_tensor(in_local[b][:], rows_t[1][b][:, :, D + 1], base[:], ALU.subtract).then_inc(local_ready, 1)
                dve.wait_ge(local_ready, m * 2 + 1)
                nc.vector.tensor_scalar(base[:], base[:], float(MACRO), None, ALU.add).then_inc(local_ready, 1)
                if not first:
                    dve.wait_ge(agg_ready, m - 1)
                nc.vector.tensor_tensor(hot[1][b][:], iota_row[:].unsqueeze(1).to_broadcast([P, 4, P]), in_local[b][:].unsqueeze(2).to_broadcast([P, 4, P]), ALU.is_equal)
                nc.vector.tensor_tensor(hot[0][b][:], iota_row[:].unsqueeze(1).to_broadcast([P, 4, P]), rows_t[0][b][:, :, D].unsqueeze(2).to_broadcast([P, 4, P]), ALU.is_equal).then_inc(hot_ready, 1)
                dve.wait_ge(local_ready, m * 2 + 2)

            def agg_copy(k, b):
                m = k * 2 + b
                dve.wait_ge(agg_ready, m + 1)
                nc.vector.tensor_copy(agg_T[b][:], ps_agg[:]).then_inc(agg_copied, 1)

            def norm(k, b, first=False):
                m = k * 2 + b
                dve.wait_ge(y_ready, m + 1)
                dve.wait_ge(xb_ready, m + 1)
                nc.vector.tensor_tensor(res[b][:], ps_y[b][:, :, 0:D], xb[b][:], ALU.add).then_inc(res_ready, 1)
                dve.wait_ge(res_ready, m + 1)
                for j in range(4):
                    last = nc.vector.bn_stats(stats[b][:, j, :], res[b][:, j, :])
                last.then_inc(stats_ready, 1)
                dve.wait_ge(stats_ready, m + 1)
                nc.vector.tensor_tensor(both[b][:], stats[b][:, :, 1:3], stats[b][:, :, 4:6], ALU.add).then_inc(mv_chain, 1)
                nc.vector.tensor_tensor(apart[b][:], stats[b][:, :, 1], stats[b][:, :, 4], ALU.subtract).then_inc(mv_chain, 1)
                dve.wait_ge(mv_chain, m * 4 + 2)
                nc.vector.scalar_tensor_tensor(out=apart_sq[b][:], in0=apart[b][:], scalar=D / 4.0, in1=apart[b][:], op0=ALU.mult, op1=ALU.mult).then_inc(mv_chain, 1)
                nc.vector.tensor_scalar(mean[b][:], both[b][:, :, 0], 0.5, None, ALU.mult).then_inc(mv_chain, 1)
                dve.wait_ge(mv_chain, m * 4 + 4)
                nc.vector.tensor_tensor(var_d[b][:], both[b][:, :, 1], apart_sq[b][:], ALU.add).then_inc(mv_ready, 1)
                dve.wait_ge(std_ready, m + 1)
                nc.vector.reciprocal(rstd[b][:], std[b][:]).then_inc(rstd_ready, 1)
                dve.wait_ge(rstd_ready, m + 1)
                if not first:
                    dve.wait_ge(stored[b], k * 16)
                for j in range(4):
                    last = nc.vector.tensor_scalar(y_t[b][:, j, :], res[b][:, j, :], mean[b][:, j:j + 1], rstd[b][:, j:j + 1], ALU.subtract, ALU.mult)
                last.then_inc(y_done, 1)

            hots(0, 0, True)
            hots(0, 1, True)
            agg_copy(0, 0)
            for b in range(2):
                hots(1, b)
                agg_copy(b, 1 - b)
                norm(0, b, True)
            with dve.Fori(2, HALF) as k:
                for b in range(2):
                    hots(k, b)
                    agg_copy(k - 1 + b, 1 - b)
                    norm(k - 1, b)
            agg_copy(HALF - 1, 1)
            norm(HALF - 1, 0)
            norm(HALF - 1, 1)

        @block.scalar
        def _(act):
            act.wait_ge(consts, 9)
            with act.Fori(0, ET) as t:
                for j in range(2):
                    act.wait_ge(sums_ready[j], t + 1)
                    act.wait_ge(table_settled[j], t * 16 + INIT)
                    nc.scalar.copy(stage[j][:, 0:D], ps_hid[j][:, 1, 0:D]).then_inc(stage_ready[j], 1)
            act.wait_ge(weights_in, 6 * 16)

            def x_copy(k, b):
                m = k * 2 + b
                act.wait_ge(xT_ready, m + 1)
                nc.scalar.copy(x_T[b][:], ps_x[:, 0:2, :]).then_inc(xT_copied, 1)

            def relu(k, b):
                m = k * 2 + b
                act.wait_ge(hid_ready, m + 1)
                for c in range(2):
                    last = nc.scalar.activation(hid[b][:, c, :], ps_hid[b][:, c, :], ACT.Relu, bias=b_1[:, c:c + 1])
                last.then_inc(relu_done, 1)

            def stds(k, b):
                m = k * 2 + b
                act.wait_ge(mv_ready, m + 1)
                nc.scalar.activation(std[b][:], var_d[b][:], ACT.Sqrt, bias=eps[:], scale=1.0 / D).then_inc(std_ready, 1)

            x_copy(0, 0)
            x_copy(0, 1)
            relu(0, 0)
            with act.Fori(1, HALF) as k:
                for b in range(2):
                    x_copy(k, b)
                    relu(k - 1 + b, 1 - b)
                    stds(k - 1, b)
            relu(HALF - 1, 1)
            stds(HALF - 1, 0)
            stds(HALF - 1, 1)

        @block.tensor
        def _(pe):
            pe.wait_ge(consts, 9)
            with pe.Fori(0, ET) as t:
                for j in range(2):
                    pe.wait_ge(idx_wide_ready[j], t + 1)
                    nc.tensor.transpose(ps_hid[j][:, 0, 0:P], idx_wide[j][:], ident[:]).then_inc(idx_row_ready[j], 1)
                for j in range(2):
                    pe.wait_ge(same_ready[j], t + 1)
                    nc.tensor.matmul(ps_hid[j][:, 1, 0:D], same[j][:], edges[:, bass.ds(t, 1), :].rearrange("p o d -> p (o d)"), start=True, stop=True).then_inc(sums_ready[j], 1)
                for j in range(2):
                    pe.wait_ge(stage_ready[j], t + 1)
            pe.wait_ge(weights_in, 6 * 16)

            def gather(k, b, first=False):
                m = k * 2 + b
                pe.wait_ge(x_in[b], k * 16 + 16)
                if not first:
                    pe.wait_ge(xT_copied, m)
                for q in range(2):
                    mm = nc.tensor.transpose(ps_x[:, q, :], x_t[b][:, 2 * q:2 * q + 2, :].rearrange("p j d -> p (j d)"), ident[:])
                mm.then_inc(xT_ready, 1)
                pe.wait_ge(hot_ready, m + 1)
                if not first:
                    pe.wait_ge(agg_copied, m)
                for j in range(4):
                    for side in range(2):
                        half = slice(D, P) if side == 0 else slice(0, D)
                        mm = nc.tensor.matmul(ps_agg[half, j * P:(j + 1) * P], rows_t[side][b][:, j, 0:D], hot[side][b][:, j, :], start=True, stop=True)
                mm.then_inc(agg_ready, 1)

            def agg_part(b, c):
                nc.tensor.matmul(ps_hid[b][:, c, :], w_agg[:, c * P:(c + 1) * P], agg_T[b][:], start=True, stop=False)

            def x_part(b, c, half, stop):
                rows = slice(half * D, (half + 1) * D)
                tiles = ps_hid[b][:, c, :].rearrange("p (q half n) -> p half q n", q=2, half=2)[:, half]
                return nc.tensor.matmul(tiles, w_x[rows, c * P:(c + 1) * P], x_T[b][rows], start=False, stop=stop)

            def layer1_start(k, b):
                m = k * 2 + b
                pe.wait_ge(agg_copied, m + 1)
                pe.wait_ge(xT_copied, m + 1)
                agg_part(b, 0)
                agg_part(b, 1)
                x_part(b, 0, 0, False)
                x_part(b, 1, 1, False).then_inc(hid_crossed, 1)

            def layer1_end(k, b):
                m = k * 2 + b
                pe.wait_ge(hid_crossed, m + 1)
                x_part(b, 1, 0, True)
                x_part(b, 0, 1, True).then_inc(hid_ready, 1)

            def layer2(k, b, first=False):
                m = k * 2 + b
                pe.wait_ge(relu_done, m + 1)
                if not first:
                    pe.wait_ge(res_ready, m - 1)
                for j in range(4):
                    for c in range(2):
                        mm = nc.tensor.matmul(ps_y[b][:, j, 0:D], hid[b][:, c, j * P:(j + 1) * P], w_2[:, c, :], start=(c == 0), stop=(c == 1))
                mm.then_inc(y_ready, 1)

            gather(0, 0, True)
            gather(0, 1)
            layer1_start(0, 0)
            layer1_end(0, 0)
            for b in range(2):
                gather(1, b)
                layer1_start(b, 1 - b)
                layer2(0, b, True)
                layer1_end(b, 1 - b)
            with pe.Fori(2, HALF) as k:
                for b in range(2):
                    gather(k, b)
                    layer1_start(k - 1 + b, 1 - b)
                    layer2(k - 1, b)
                    layer1_end(k - 1 + b, 1 - b)
            layer1_start(HALF - 1, 1)
            layer2(HALF - 1, 0)
            layer1_end(HALF - 1, 1)
            layer2(HALF - 1, 1)


def kernel(x, src, dst, edge_attr_64, L0_gnn_W1, L0_gnn_b1, L0_gnn_W2, L0_gnn_b2):
    import numpy as np
    import concourse.bacc as bacc
    from concourse.bass_utils import run_bass_kernel_spmd

    def padded(a, rows, value):
        a = np.asarray(a)
        return np.concatenate([a, np.full((rows - a.shape[0],) + a.shape[1:], value, a.dtype)])

    arrays = {
        "x": padded(x, N_PAD, 0), "src": padded(src, E_PAD, N_PAD - 1), "dst": padded(dst, E_PAD, N_PAD - 1),
        "edge": padded(edge_attr_64, E_PAD, 0), "w1": np.asarray(L0_gnn_W1), "b1": np.asarray(L0_gnn_b1),
        "w2": np.asarray(L0_gnn_W2), "b2": np.asarray(L0_gnn_b2),
    }
    nc = bacc.Bacc("TRN2", target_bir_lowering=False, num_devices=1)
    args = [nc.dram_tensor(f"{n}_dram", a.shape, mybir.dt.from_np(a.dtype), kind="ExternalInput").ap() for n, a in arrays.items()]
    result = nc.dram_tensor("out_dram", (N_PAD, D), F32, kind="ExternalOutput").ap()
    gnn_kernel(nc, *args, result)
    r = run_bass_kernel_spmd(nc, [{f"{n}_dram": a for n, a in arrays.items()}], core_ids=[0])
    return r.results[0]["out_dram"][:N_NODES]
```

```python
import concourse.bass as bass
from concourse import mybir
from contextlib import ExitStack

ALU = mybir.AluOpType
ACT = mybir.ActivationFunctionType
F32 = mybir.dt.float32
F16 = mybir.dt.float16
I32 = mybir.dt.int32
AX_X = mybir.AxisListType.X

P = 128
D = 64
H = 256
N_NODES = 50000
N_EDGES = 25000
MACRO = 4 * P
MACROS = 98
N_PAD = MACROS * MACRO
BINS = N_PAD // P
ET = -(-N_EDGES // P)
E_PAD = ET * P
ROW = D + 2
TRASH = N_PAD
EPS = 1e-5
STEP = 4
STEPS = ET // STEP


def gnn_kernel(nc, x, x_cols, src, dst, dst_next, edge, w1, b1, w2, b2, out):
    in_rows = nc.dram_tensor("in_rows", [N_PAD + P, ROW], F32)
    out_rows = nc.dram_tensor("out_rows", [N_PAD + E_PAD, ROW], F32)
    tables = [out_rows, in_rows]
    with ExitStack() as ctx:
        def sb(name, shape, dt=F32):
            return ctx.enter_context(nc.sbuf_tensor(name, shape, dt))

        def psum(name, shape, dt=F32):
            return ctx.enter_context(nc.psum_tensor(name, shape, dt))

        def sem(name):
            return ctx.enter_context(nc.semaphore(name))

        ident = sb("ident", [P, P])
        earlier = sb("earlier", [P, P])
        iota_row = sb("iota_row", [P, P])
        w_agg = sb("w_agg", [P, H])
        w_x = sb("w_x", [P, H])
        w_2 = sb("w_2", [P, 2, D])
        b_1 = sb("b_1", [P, 2])
        b_2 = sb("b_2", [P, D])
        eps = sb("eps", [P, 1])
        packed = sb("packed", [P, ET, ROW])
        ends_i = sb("ends_i", [P, 3, ET], I32)
        bins_i = sb("bins_i", [P, 3, ET], I32)
        ends = sb("ends", [P, 3, ET])
        bins = sb("bins", [P, 2, ET])
        bin_base = sb("bin_base", [P, ET])
        fall = sb("fall", [P, ET])
        bin_iota = sb("bin_iota", [P, BINS], F16)
        before = sb("before", [P, P], F16)
        not_before = sb("not_before", [P, P], F16)
        ones = sb("ones", [P, P], F16)
        bin_hot = [sb(f"bin_hot{i}", [P, BINS], F16) for i in range(STEP)]
        bin_above = [sb(f"bin_above{i}", [P, BINS], F16) for i in range(STEP)]
        bin_junk = [sb(f"bin_junk{i}", [P, BINS]) for i in range(STEP)]
        rank = [sb(f"rank{i}", [P, 1]) for i in range(STEP)]
        slot = [sb(f"slot{i}", [P, 1], I32) for i in range(STEP)]
        staged_rows = [sb(f"staged_rows{i}", [P, ROW]) for i in range(STEP)]
        ranks = sb("ranks", [P, ET])
        worst = sb("worst", [P, 3])
        worst_wide = sb("worst_wide", [P, P])
        first_edge = sb("first_edge", [1, BINS + 1])
        sizes = sb("sizes", [1, BINS])
        verdict = sb("verdict", [1, 3])
        unfit = sb("unfit", [1, 1], I32)
        window_start = sb("window_start", [1, BINS], I32)
        init = sb("init", [P, BINS // 4, ROW])
        trash_row = sb("trash_row", [P, 1])
        idx_wide = [sb(f"idx_wide{j}", [P, P]) for j in range(2)]
        same = [sb(f"same{j}", [P, P]) for j in range(2)]
        junk = sb("junk", [P, P])
        dup = [sb(f"dup{j}", [P, 4]) for j in range(2)]
        row_index = [sb(f"row_index{j}", [P, 1], I32) for j in range(2)]
        stage = [sb(f"stage{j}", [P, ROW]) for j in range(2)]
        x_t = [sb(f"x_t{b}", [P, 4, D]) for b in range(2)]
        rows_t = [[sb(f"rows_t{j}{b}", [P, 4, ROW]) for b in range(2)] for j in range(2)]
        base = sb("base", [P, 4])
        in_local = [sb(f"in_local{b}", [P, 4]) for b in range(2)]
        hot = [[sb(f"hot{j}{b}", [P, 4, P]) for b in range(2)] for j in range(2)]
        agg_T = [sb(f"agg_T{b}", [P, MACRO]) for b in range(2)]
        x_T = [sb(f"x_T{b}", [P, MACRO // 2]) for b in range(2)]
        hid = [sb(f"hid{b}", [P, 2, MACRO]) for b in range(2)]
        xb = [sb(f"xb{b}", [P, 4, D]) for b in range(2)]
        res = [sb(f"res{b}", [P, 4, D]) for b in range(2)]
        stats = [sb(f"stats{b}", [P, 4, 6]) for b in range(2)]
        both = [sb(f"both{b}", [P, 4, 2]) for b in range(2)]
        apart = [sb(f"apart{b}", [P, 4]) for b in range(2)]
        apart_sq = [sb(f"apart_sq{b}", [P, 4]) for b in range(2)]
        mean = [sb(f"mean{b}", [P, 4]) for b in range(2)]
        var_d = [sb(f"var_d{b}", [P, 4]) for b in range(2)]
        std = [sb(f"std{b}", [P, 4]) for b in range(2)]
        rstd = [sb(f"rstd{b}", [P, 4]) for b in range(2)]
        y_t = [sb(f"y_t{b}", [P, 4, D]) for b in range(2)]

        ps_agg = [psum(f"ps_agg{b}", [P, MACRO]) for b in range(2)]
        ps_hid = [psum(f"ps_hid{b}", [P, 2, MACRO]) for b in range(2)]
        ps_y = [psum(f"ps_y{b}", [P, 4 * P]) for b in range(2)]

        weights_in = sem("weights_in")
        ends_in = sem("ends_in")
        edges_in = sem("edges_in")
        zeros_made = sem("zeros_made")
        out_zeroed = sem("out_zeroed")
        packed_ready = sem("packed_ready")
        in_stored = sem("in_stored")
        prep_chain = sem("prep_chain")
        triangles = sem("triangles")
        hot_made = sem("hot_made")
        ranked = sem("ranked")
        pair_counted = sem("pair_counted")
        rank_read = sem("rank_read")
        rank_kept = sem("rank_kept")
        staged = sem("staged")
        slot_made = sem("slot_made")
        scatters_begun = sem("scatters_begun")
        scattered = [sem(f"scattered{i}") for i in range(STEP)]
        worst_ready = sem("worst_ready")
        worst_turned = sem("worst_turned")
        verdict_chain = sem("verdict_chain")
        unfit_ready = sem("unfit_ready")
        tables_ready = sem("tables_ready")
        consts = sem("consts")
        init_made = sem("init_made")
        table_settled = [sem("out_settled"), sem("in_settled")]
        idx_wide_ready = [sem(f"idx_wide_ready{j}") for j in range(2)]
        idx_row_ready = [sem(f"idx_row_ready{j}") for j in range(2)]
        same_ready = [sem(f"same_ready{j}") for j in range(2)]
        dup_chain = [sem(f"dup_chain{j}") for j in range(2)]
        additions_begun = sem("additions_begun")
        sums_ready = [sem(f"sums_ready{j}") for j in range(2)]
        stage_ready = [sem(f"stage_ready{j}") for j in range(2)]
        x_in = [sem(f"x_in{b}") for b in range(2)]
        rows_in = [sem(f"rows_in{b}") for b in range(2)]
        local_ready = sem("local_ready")
        hot_ready = sem("hot_ready")
        agg_ready = sem("agg_ready")
        agg_copied = sem("agg_copied")
        hid_crossed = sem("hid_crossed")
        hid_ready = sem("hid_ready")
        relu_done = sem("relu_done")
        y_ready = sem("y_ready")
        xb_ready = sem("xb_ready")
        res_ready = sem("res_ready")
        stats_ready = sem("stats_ready")
        mv_chain = sem("mv_chain")
        mv_ready = sem("mv_ready")
        std_ready = sem("std_ready")
        rstd_ready = sem("rstd_ready")
        y_done = sem("y_done")
        stored = [sem(f"stored{b}") for b in range(2)]

        INIT = 5 * 16
        HALF = MACROS // 2

        block = ctx.enter_context(nc.Block())

        @block.sync
        def _(sp):
            for k, e in enumerate((src, dst, dst_next)):
                sp.dma_start(ends_i[:, k, :], e.rearrange("(p t) -> p t", p=P)).then_inc(ends_in, 16)
            sp.dma_start(packed[:, :, 0:D], edge.rearrange("(p t) d -> p t d", p=P)).then_inc(edges_in, 16)
            sp.dma_start(w_agg[:], w1[0:P, :]).then_inc(weights_in, 16)
            for half in range(2):
                sp.dma_start(w_x[half * D:(half + 1) * D, :], w1[P:P + D, :]).then_inc(weights_in, 16)
            sp.dma_start(w_2[:], w2.rearrange("(c p) d -> p c d", p=P)).then_inc(weights_in, 16)
            with nc.allow_non_contiguous_dma(reason="256 values"):
                sp.dma_start(b_1[:], b1.rearrange("(c p) -> p c", p=P)).then_inc(weights_in, 16)
            sp.dma_start(b_2[:], b2.rearrange("(o d) -> o d", o=1).to_broadcast([P, D])).then_inc(weights_in, 16)

            sp.wait_ge(packed_ready, 2)
            sp.wait_ge(edges_in, 16)
            sp.dma_start(in_rows[0:E_PAD, :].rearrange("(p t) d -> p (t d)", p=P), packed[:].rearrange("p t d -> p (t d)")).then_inc(in_stored, 16)

            sp.wait_ge(unfit_ready, 1)
            sp.wait_ge(tables_ready, 1)
            sp.wait_ge(in_stored, 16)

            def load_rows(k, b, first=False):
                m = k * 2 + b
                if not first:
                    sp.wait_ge(agg_ready, m - 1)
                    sp.wait_ge(hot_ready, m - 1)
                starts = nc.values_load_multi_w_load_instructions(window_start[0:1, bass.ds(m * 4, 4)], engines=(mybir.EngineType.SP,), min_val=0, max_val=N_PAD - P)[1]
                sp.dma_start(rows_t[0][b][:], out_rows[bass.ds(m * MACRO, MACRO), :].rearrange("(j p) d -> p j d", p=P)).then_inc(rows_in[b], 16)
                for j in range(4):
                    sp.dma_start(rows_t[1][b][:, j, :], in_rows[bass.ds(starts[j], P), :]).then_inc(rows_in[b], 16)

            def load_x(k, b, first=False):
                m = k * 2 + b
                if not first:
                    sp.wait_ge(hid_ready, m - 1)
                    sp.wait_ge(xb_ready, m - 1)
                sp.dma_start(x_T[b][:], x_cols[:, bass.ds(m * (MACRO // 2), MACRO // 2)]).then_inc(x_in[b], 16)
                sp.dma_start(x_t[b][:], x[bass.ds(m * MACRO, MACRO), :].rearrange("(j p) d -> p j d", p=P)).then_inc(x_in[b], 16)

            load_rows(0, 0, True)
            load_rows(0, 1, True)
            load_x(0, 0, True)
            load_rows(1, 0)
            load_x(0, 1, True)
            load_rows(1, 1)
            with sp.Fori(1, HALF - 1) as k:
                load_x(k, 0)
                load_rows(k + 1, 0)
                load_x(k, 1)
                load_rows(k + 1, 1)
            load_x(HALF - 1, 0)
            load_x(HALF - 1, 1)

        @block.gpsimd
        def _(pool):
            nc.gpsimd.memset(ident[:], 0.0).then_inc(init_made, 1)
            nc.gpsimd.memset(earlier[:], 1.0).then_inc(init_made, 1)
            nc.gpsimd.memset(before[:], 1.0).then_inc(init_made, 1)
            nc.gpsimd.memset(not_before[:], 1.0).then_inc(init_made, 1)
            nc.gpsimd.memset(ones[:], 1.0).then_inc(triangles, 1)
            nc.gpsimd.iota(bin_iota[:], [[1, BINS]], base=0, channel_multiplier=0, allow_small_or_imprecise_dtypes=True).then_inc(triangles, 1)
            pool.wait_ge(init_made, 4)
            nc.gpsimd.affine_select(out=before[:], in_=before[:], compare_op=ALU.is_gt, fill=0.0, base=0, pattern=[[1, P]], channel_multiplier=-1).then_inc(triangles, 1)
            nc.gpsimd.affine_select(out=not_before[:], in_=not_before[:], compare_op=ALU.is_ge, fill=0.0, base=0, pattern=[[-1, P]], channel_multiplier=1).then_inc(triangles, 1)
            nc.gpsimd.affine_select(out=ident[:], in_=ident[:], compare_op=ALU.not_equal, fill=1.0, base=0, pattern=[[-1, P]], channel_multiplier=1).then_inc(consts, 1)
            nc.gpsimd.affine_select(out=earlier[:], in_=earlier[:], compare_op=ALU.is_gt, fill=0.0, base=0, pattern=[[-1, P]], channel_multiplier=1).then_inc(consts, 1)
            nc.gpsimd.memset(eps[:], EPS).then_inc(consts, 1)
            nc.gpsimd.memset(stage[0][:], 0.0).then_inc(consts, 1)
            nc.gpsimd.memset(stage[1][:], 0.0).then_inc(consts, 1)
            nc.gpsimd.iota(iota_row[:], [[1, P]], base=0, channel_multiplier=0, allow_small_or_imprecise_dtypes=True).then_inc(consts, 1)
            nc.gpsimd.iota(base[:], [[P, 4]], base=0, channel_multiplier=0, allow_small_or_imprecise_dtypes=True).then_inc(consts, 1)
            nc.gpsimd.iota(trash_row[:], [[0, 1]], base=TRASH, channel_multiplier=1, allow_small_or_imprecise_dtypes=True).then_inc(consts, 1)

            def scatter(u, i):
                t = u * STEP + i
                pool.wait_ge(staged, t + 1)
                pool.wait_ge(slot_made, t + 1)
                pool.sem_inc(scatters_begun, 1)
                nc.gpsimd.indirect_dma_start(
                    out=out_rows[:, :], out_offset=bass.IndirectOffsetOnAxis(ap=slot[i][:], axis=0),
                    in_=staged_rows[i][:], in_offset=None).then_inc(scattered[i], 16)

            pool.wait_ge(out_zeroed, 4 * 16)
            with pool.Fori(0, STEPS) as u:
                for i in range(STEP):
                    scatter(u, i)
            for i in range(STEP):
                pool.wait_ge(scattered[i], 16 * STEPS)
            pool.wait_ge(in_stored, 16)

            def add_all():
                nc.gpsimd.iota(init[:, :, D:D + 1], [[0, BINS // 4]], base=0, channel_multiplier=1, allow_small_or_imprecise_dtypes=True).then_inc(init_made, 1)
                nc.gpsimd.iota(window_start[:], [[P, BINS]], base=0, channel_multiplier=0).then_inc(init_made, 1)
                for q in range(4):
                    lo = q * (BINS // 4) * P
                    if q:
                        for j in range(2):
                            pool.wait_ge(table_settled[j], 16 * q)
                    nc.gpsimd.iota(init[:, :, D + 1:D + 2], [[P, BINS // 4]], base=lo, channel_multiplier=1, allow_small_or_imprecise_dtypes=True).then_inc(init_made, 1)
                    pool.wait_ge(init_made, 7 + q)
                    for j in range(2):
                        pool.dma_start(tables[j][lo:lo + (BINS // 4) * P, :].rearrange("(c p) d -> p c d", p=P), init[:]).then_inc(table_settled[j], 16)
                for j in range(2):
                    pool.dma_start(tables[j][TRASH:TRASH + P, :], init[:, 0, :]).then_inc(table_settled[j], 16)
                with pool.Fori(0, ET) as t:
                    for j in range(2):
                        pool.wait_ge(stage_ready[j], t + 1)
                        pool.wait_ge(dup_chain[j], t * 4 + 4)
                        pool.wait_ge(table_settled[j], t * 16 + INIT)
                        pool.sem_inc(additions_begun, 1)
                        nc.gpsimd.indirect_dma_start(
                            out=tables[j][:, :], out_offset=bass.IndirectOffsetOnAxis(ap=row_index[j][:], axis=0),
                            in_=stage[j][:], in_offset=None, compute_op=ALU.add).then_inc(table_settled[j], 16)
                for j in range(2):
                    pool.wait_ge(table_settled[j], INIT + 16 * ET)

            pool.wait_ge(unfit_ready, 1)
            with pool.If(pool.value_load(unfit[0:1, 0:1], min_val=0, max_val=1) > 0):
                add_all()
            pool.sem_inc(tables_ready, 1)

            pool.wait_ge(weights_in, 6 * 16)

            def step(k, b, first=False):
                m = k * 2 + b
                pool.wait_ge(x_in[b], k * 32 + 32)
                if not first:
                    pool.wait_ge(res_ready, m - 1)
                nc.gpsimd.tensor_tensor(xb[b][:], x_t[b][:], b_2[:].unsqueeze(1).to_broadcast([P, 4, D]), ALU.add).then_inc(xb_ready, 1)

            def store(k, b):
                m = k * 2 + b
                pool.wait_ge(y_done, m + 1)
                pool.dma_start(out[bass.ds(m * MACRO, MACRO), :].rearrange("(j p) d -> p j d", p=P), y_t[b][:]).then_inc(stored[b], 16)

            step(0, 0, True)
            step(0, 1, True)
            with pool.Fori(1, HALF) as k:
                for b in range(2):
                    step(k, b)
                    store(k - 1, b)
            for b in range(2):
                store(HALF - 1, b)
            for b in range(2):
                pool.wait_ge(stored[b], 16 * HALF)

        @block.vector
        def _(dve):
            nc.vector.memset(init[:], 0.0).then_inc(zeros_made, 1)
            nc.vector.memset(first_edge[0:1, BINS:BINS + 1], float(E_PAD)).then_inc(verdict_chain, 1)
            dve.wait_ge(ends_in, 3 * 16)
            nc.vector.tensor_scalar(bins_i[:, 0:2, :], ends_i[:, 0:2, :], 7, None, ALU.logical_shift_right).then_inc(prep_chain, 1)
            nc.vector.tensor_scalar(bins_i[:, 2, :], ends_i[:, 0, :], P - 1, None, ALU.bitwise_and).then_inc(prep_chain, 1)
            nc.vector.tensor_copy(ends[:], ends_i[:]).then_inc(prep_chain, 1)
            dve.wait_ge(prep_chain, 3)
            nc.vector.tensor_copy(bins[:], bins_i[:, 0:2, :]).then_inc(prep_chain, 1)
            nc.vector.tensor_copy(packed[:, :, D], bins_i[:, 2, :]).then_inc(packed_ready, 1)
            nc.vector.tensor_copy(packed[:, :, D + 1], ends[:, 1, :]).then_inc(packed_ready, 1)
            nc.vector.tensor_tensor(fall[:], ends[:, 1, :], ends[:, 2, :], ALU.subtract).then_inc(prep_chain, 1)
            dve.wait_ge(prep_chain, 5)
            nc.vector.tensor_scalar(bin_base[:], bins[:, 0, :], float(P), None, ALU.mult).then_inc(prep_chain, 1)
            nc.vector.tensor_reduce(worst[:, 0:1], fall[:], AX_X, ALU.max).then_inc(prep_chain, 1)
            dve.wait_ge(prep_chain, 7)
            dve.wait_ge(triangles, 4)

            def bin_hots(u, q, first=False):
                if not first:
                    dve.wait_ge(pair_counted, u * 2 + (q - 1))
                for i in (2 * q, 2 * q + 1):
                    t = u * STEP + i
                    nc.vector.tensor_scalar(bin_hot[i][:], bin_iota[:], bins[:, 0, bass.ds(t, 1)], None, ALU.is_equal).then_inc(hot_made, 1)
                    nc.vector.tensor_scalar(bin_above[i][:], bin_iota[:], bins[:, 1, bass.ds(t, 1)], None, ALU.is_gt).then_inc(hot_made, 1)

            def read_ranks(u, q, first=False):
                for i in (2 * q, 2 * q + 1):
                    t = u * STEP + i
                    dve.wait_ge(ranked, t + 1)
                    if not first:
                        dve.wait_ge(rank_kept, t - 3)
                        dve.wait_ge(slot_made, t - 3)
                    nc.vector.tensor_tensor_reduce(out=bin_junk[i][:], in0=ps_y[i % 2][:, 0:BINS], in1=bin_hot[i][:], scale=1.0, scalar=0.0, op0=ALU.mult, op1=ALU.add, accum_out=rank[i][:]).then_inc(rank_read, 1)
                for i in (2 * q, 2 * q + 1):
                    t = u * STEP + i
                    dve.wait_ge(rank_read, t + 1)
                    if not first:
                        dve.wait_ge(scattered[i], u * 16)
                    nc.vector.tensor_tensor(slot[i][:], rank[i][:], bin_base[:, bass.ds(t, 1)], ALU.add).then_inc(slot_made, 1)

            bin_hots(0, 0, True)
            bin_hots(0, 1, True)
            read_ranks(0, 0, True)
            bin_hots(1, 0)
            read_ranks(0, 1, True)
            with dve.Fori(1, STEPS - 1) as u:
                bin_hots(u, 1)
                read_ranks(u, 0)
                bin_hots(u + 1, 0)
                read_ranks(u, 1)
            bin_hots(STEPS - 1, 1)
            read_ranks(STEPS - 1, 0)
            read_ranks(STEPS - 1, 1)

            dve.wait_ge(rank_kept, ET)
            nc.vector.tensor_reduce(worst[:, 1:2], ranks[:], AX_X, ALU.max).then_inc(verdict_chain, 1)
            dve.wait_ge(pair_counted, ET // 2)
            nc.vector.tensor_copy(first_edge[0:1, 0:BINS], ps_agg[0][0:1, 0:BINS]).then_inc(verdict_chain, 1)
            dve.wait_ge(verdict_chain, 3)
            nc.vector.scalar_tensor_tensor(out=worst[:, 2:3], in0=worst[:, 1:2], scalar=float(1 - P), in1=worst[:, 0:1], op0=ALU.add, op1=ALU.max).then_inc(verdict_chain, 1)
            nc.vector.tensor_tensor(sizes[:], first_edge[0:1, 1:BINS + 1], first_edge[0:1, 0:BINS], ALU.subtract).then_inc(verdict_chain, 1)
            nc.vector.tensor_scalar(window_start[:], first_edge[0:1, 0:BINS], float(E_PAD - P), None, ALU.min).then_inc(verdict_chain, 1)
            dve.wait_ge(verdict_chain, 6)
            nc.vector.tensor_copy(worst_wide[:], worst[:, 2:3].to_broadcast([P, P])).then_inc(worst_ready, 1)
            nc.vector.tensor_reduce(verdict[:, 0:1], sizes[:], AX_X, ALU.max).then_inc(verdict_chain, 1)
            dve.wait_ge(worst_turned, 1)
            nc.vector.tensor_reduce(verdict[:, 1:2], ps_hid[0][0:1, 0, 0:P], AX_X, ALU.max).then_inc(verdict_chain, 1)
            dve.wait_ge(verdict_chain, 8)
            nc.vector.scalar_tensor_tensor(out=verdict[:, 2:3], in0=verdict[:, 0:1], scalar=float(-P), in1=verdict[:, 1:2], op0=ALU.add, op1=ALU.max).then_inc(verdict_chain, 1)
            dve.wait_ge(verdict_chain, 9)
            nc.vector.tensor_scalar(unfit[:], verdict[:, 2:3], 0.0, None, ALU.is_gt).then_inc(unfit_ready, 1)

            def add_all():
                dve.wait_ge(consts, 8)
                with dve.Fori(0, ET) as t:
                    for j in range(2):
                        nc.vector.tensor_copy(idx_wide[j][:], ends[:, j, bass.ds(t, 1)].to_broadcast([P, P])).then_inc(idx_wide_ready[j], 1)
                    for j in range(2):
                        dve.wait_ge(idx_row_ready[j], t + 1)
                        nc.vector.tensor_scalar(same[j][:], ps_hid[j][:, 0, 0:P], idx_wide[j][:, 0:1], None, ALU.is_equal).then_inc(same_ready[j], 1)
                        dve.wait_ge(same_ready[j], t + 1)
                        nc.vector.tensor_tensor_reduce(out=junk[:], in0=same[j][:], in1=earlier[:], scale=1.0, scalar=0.0, op0=ALU.mult, op1=ALU.add, accum_out=dup[j][:, 0:1]).then_inc(dup_chain[j], 1)
                        nc.vector.tensor_tensor(dup[j][:, 1:2], trash_row[:], idx_wide[j][:, 0:1], ALU.subtract).then_inc(dup_chain[j], 1)
                        dve.wait_ge(dup_chain[j], t * 4 + 2)
                        nc.vector.tensor_scalar(dup[j][:, 2:3], dup[j][:, 0:1], 1.0, dup[j][:, 1:2], ALU.min, ALU.mult).then_inc(dup_chain[j], 1)
                        dve.wait_ge(dup_chain[j], t * 4 + 3)
                        dve.wait_ge(table_settled[j], t * 16 + INIT)
                        nc.vector.tensor_tensor(row_index[j][:], dup[j][:, 2:3], idx_wide[j][:, 0:1], ALU.add).then_inc(dup_chain[j], 1)
                        dve.wait_ge(dup_chain[j], t * 4 + 4)

            dve.wait_ge(unfit_ready, 1)
            with dve.If(dve.value_load(unfit[0:1, 0:1], min_val=0, max_val=1) > 0):
                add_all()
            dve.wait_ge(consts, 8)

            def hots(k, b, first=False):
                m = k * 2 + b
                dve.wait_ge(rows_in[b], k * 80 + 80)
                nc.vector.tensor_tensor(in_local[b][:], rows_t[1][b][:, :, D + 1], base[:], ALU.subtract).then_inc(local_ready, 1)
                dve.wait_ge(local_ready, m * 2 + 1)
                nc.vector.tensor_scalar(base[:], base[:], float(MACRO), None, ALU.add).then_inc(local_ready, 1)
                if not first:
                    dve.wait_ge(agg_ready, m - 1)
                nc.vector.tensor_tensor(hot[1][b][:], iota_row[:].unsqueeze(1).to_broadcast([P, 4, P]), in_local[b][:].unsqueeze(2).to_broadcast([P, 4, P]), ALU.is_equal)
                nc.vector.tensor_tensor(hot[0][b][:], iota_row[:].unsqueeze(1).to_broadcast([P, 4, P]), rows_t[0][b][:, :, D].unsqueeze(2).to_broadcast([P, 4, P]), ALU.is_equal).then_inc(hot_ready, 1)
                dve.wait_ge(local_ready, m * 2 + 2)

            def agg_copy(k, b):
                m = k * 2 + b
                dve.wait_ge(agg_ready, m + 1)
                nc.vector.tensor_copy(agg_T[b][:], ps_agg[b][:]).then_inc(agg_copied, 1)

            def norm(k, b, first=False):
                m = k * 2 + b
                dve.wait_ge(y_ready, m + 1)
                dve.wait_ge(xb_ready, m + 1)
                nc.vector.tensor_tensor(res[b][:], ps_y[b][:, 0:4 * D].rearrange("p (j d) -> p j d", j=4), xb[b][:], ALU.add).then_inc(res_ready, 1)
                dve.wait_ge(res_ready, m + 1)
                for j in range(4):
                    last = nc.vector.bn_stats(stats[b][:, j, :], res[b][:, j, :])
                last.then_inc(stats_ready, 1)
                dve.wait_ge(stats_ready, m + 1)
                nc.vector.tensor_tensor(both[b][:], stats[b][:, :, 1:3], stats[b][:, :, 4:6], ALU.add).then_inc(mv_chain, 1)
                nc.vector.tensor_tensor(apart[b][:], stats[b][:, :, 1], stats[b][:, :, 4], ALU.subtract).then_inc(mv_chain, 1)
                dve.wait_ge(mv_chain, m * 4 + 2)
                nc.vector.scalar_tensor_tensor(out=apart_sq[b][:], in0=apart[b][:], scalar=D / 4.0, in1=apart[b][:], op0=ALU.mult, op1=ALU.mult).then_inc(mv_chain, 1)
                nc.vector.tensor_scalar(mean[b][:], both[b][:, :, 0], 0.5, None, ALU.mult).then_inc(mv_chain, 1)
                dve.wait_ge(mv_chain, m * 4 + 4)
                nc.vector.tensor_tensor(var_d[b][:], both[b][:, :, 1], apart_sq[b][:], ALU.add).then_inc(mv_ready, 1)
                dve.wait_ge(std_ready, m + 1)
                nc.vector.reciprocal(rstd[b][:], std[b][:]).then_inc(rstd_ready, 1)
                dve.wait_ge(rstd_ready, m + 1)
                if not first:
                    dve.wait_ge(stored[b], k * 16)
                for j in range(4):
                    last = nc.vector.tensor_scalar(y_t[b][:, j, :], res[b][:, j, :], mean[b][:, j:j + 1], rstd[b][:, j:j + 1], ALU.subtract, ALU.mult)
                last.then_inc(y_done, 1)

            hots(0, 0, True)
            agg_copy(0, 0)
            hots(0, 1, True)
            agg_copy(0, 1)
            hots(1, 0)
            for b in range(2):
                agg_copy(1, b)
                hots(1 + b, 1 - b)
                norm(0, b, True)
            with dve.Fori(2, HALF - 1) as k:
                for b in range(2):
                    agg_copy(k, b)
                    hots(k + b, 1 - b)
                    norm(k - 1, b)
            agg_copy(HALF - 1, 0)
            hots(HALF - 1, 1)
            norm(HALF - 2, 0)
            agg_copy(HALF - 1, 1)
            norm(HALF - 2, 1)
            norm(HALF - 1, 0)
            norm(HALF - 1, 1)

        @block.scalar
        def _(act):
            act.wait_ge(zeros_made, 1)
            quarter = BINS // 4 * P
            for q in range(4):
                act.dma_start(out_rows[q * quarter:(q + 1) * quarter, :].rearrange("(p c) d -> p (c d)", p=P), init[:].rearrange("p c d -> p (c d)")).then_inc(out_zeroed, 16)
            nc.scalar.preload_act_table(ACT.Sqrt)
            act.wait_ge(packed_ready, 2)
            act.wait_ge(edges_in, 16)

            def stage_rows(u, i, first=False):
                t = u * STEP + i
                if not first:
                    act.wait_ge(scattered[i], u * 16)
                nc.scalar.copy(staged_rows[i][:], packed[:, bass.ds(t, 1), :].rearrange("p o d -> p (o d)")).then_inc(staged, 1)
                act.wait_ge(rank_read, t + 1)
                nc.scalar.copy(ranks[:, bass.ds(t, 1)], rank[i][:]).then_inc(rank_kept, 1)

            for i in range(STEP):
                stage_rows(0, i, True)
            with act.Fori(1, STEPS) as u:
                for i in range(STEP):
                    stage_rows(u, i)

            def add_all():
                with act.Fori(0, ET) as t:
                    for j in range(2):
                        act.wait_ge(sums_ready[j], t + 1)
                        act.wait_ge(table_settled[j], t * 16 + INIT)
                        nc.scalar.copy(stage[j][:, 0:D], ps_hid[j][:, 1, 0:D]).then_inc(stage_ready[j], 1)

            act.wait_ge(unfit_ready, 1)
            with act.If(act.value_load(unfit[0:1, 0:1], min_val=0, max_val=1) > 0):
                add_all()
            act.wait_ge(consts, 8)
            act.wait_ge(weights_in, 6 * 16)

            def relu(k, b):
                m = k * 2 + b
                act.wait_ge(hid_ready, m + 1)
                for c in range(2):
                    last = nc.scalar.activation(hid[b][:, c, :], ps_hid[b][:, c, :], ACT.Relu, bias=b_1[:, c:c + 1])
                last.then_inc(relu_done, 1)

            def stds(k, b):
                m = k * 2 + b
                act.wait_ge(mv_ready, m + 1)
                nc.scalar.activation(std[b][:], var_d[b][:], ACT.Sqrt, bias=eps[:], scale=1.0 / D).then_inc(std_ready, 1)

            relu(0, 0)
            with act.Fori(1, HALF) as k:
                for b in range(2):
                    stds(k - 1, b)
                    relu(k - 1 + b, 1 - b)
            stds(HALF - 1, 0)
            relu(HALF - 1, 1)
            stds(HALF - 1, 1)

        @block.tensor
        def _(pe):
            def count(bank, lhsT, rhs, start=False):
                return nc.tensor.matmul(bank, lhsT, rhs, start=start, stop=True, skip_group_check=True)

            def rank_pair(u, q, first=False):
                even, odd = 2 * q, 2 * q + 1
                t = u * STEP + even
                pe.wait_ge(hot_made, t * 2 + 4)
                count(ps_y[0][:, 0:BINS], before[:], bin_hot[even][:], first).then_inc(ranked, 1)
                count(ps_y[1][:, 0:BINS], ones[:], bin_hot[even][:], first)
                count(ps_y[1][:, 0:BINS], before[:], bin_hot[odd][:]).then_inc(ranked, 1)
                count(ps_agg[0][0:1, 0:BINS], ones[:, 0:1], bin_above[even][:], first)
                count(ps_agg[0][0:1, 0:BINS], ones[:, 0:1], bin_above[odd][:])
                pe.wait_ge(rank_read, t + 1)
                count(ps_y[0][:, 0:BINS], not_before[:], bin_hot[even][:])
                count(ps_y[0][:, 0:BINS], ones[:], bin_hot[odd][:])
                pe.wait_ge(rank_read, t + 2)
                count(ps_y[1][:, 0:BINS], not_before[:], bin_hot[odd][:]).then_inc(pair_counted, 1)

            pe.wait_ge(triangles, 4)
            rank_pair(0, 0, True)
            rank_pair(0, 1)
            with pe.Fori(1, STEPS) as u:
                rank_pair(u, 0)
                rank_pair(u, 1)
            pe.wait_ge(consts, 8)
            pe.wait_ge(worst_ready, 1)
            nc.tensor.transpose(ps_hid[0][:, 0, 0:P], worst_wide[:], ident[:]).then_inc(worst_turned, 1)

            def add_all():
                pe.wait_ge(edges_in, 16)
                with pe.Fori(0, ET) as t:
                    for j in range(2):
                        pe.wait_ge(idx_wide_ready[j], t + 1)
                        nc.tensor.transpose(ps_hid[j][:, 0, 0:P], idx_wide[j][:], ident[:]).then_inc(idx_row_ready[j], 1)
                    for j in range(2):
                        pe.wait_ge(same_ready[j], t + 1)
                        nc.tensor.matmul(ps_hid[j][:, 1, 0:D], same[j][:], packed[:, bass.ds(t, 1), 0:D].rearrange("p o d -> p (o d)"), start=True, stop=True).then_inc(sums_ready[j], 1)
                    for j in range(2):
                        pe.wait_ge(stage_ready[j], t + 1)

            pe.wait_ge(unfit_ready, 1)
            with pe.If(pe.value_load(unfit[0:1, 0:1], min_val=0, max_val=1) > 0):
                add_all()
            pe.wait_ge(weights_in, 6 * 16)

            def gather(k, b, first=False):
                m = k * 2 + b
                pe.wait_ge(hot_ready, m + 1)
                if not first:
                    pe.wait_ge(agg_copied, m - 1)
                for j in range(4):
                    for side in range(2):
                        half = slice(D, P) if side == 0 else slice(0, D)
                        mm = nc.tensor.matmul(ps_agg[b][half, j * P:(j + 1) * P], rows_t[side][b][:, j, 0:D], hot[side][b][:, j, :], start=True, stop=True)
                mm.then_inc(agg_ready, 1)

            def agg_part(b, c):
                nc.tensor.matmul(ps_hid[b][:, c, :], w_agg[:, c * P:(c + 1) * P], agg_T[b][:], start=True, stop=False)

            def x_part(b, c, half, stop):
                rows = slice(half * D, (half + 1) * D)
                tiles = ps_hid[b][:, c, half * (MACRO // 2):(half + 1) * (MACRO // 2)]
                return nc.tensor.matmul(tiles, w_x[rows, c * P:(c + 1) * P], x_T[b][rows], start=False, stop=stop)

            def layer1_start(k, b):
                m = k * 2 + b
                pe.wait_ge(agg_copied, m + 1)
                pe.wait_ge(x_in[b], k * 32 + 32)
                agg_part(b, 0)
                agg_part(b, 1)
                x_part(b, 0, 0, False)
                x_part(b, 1, 1, False).then_inc(hid_crossed, 1)

            def layer1_end(k, b):
                m = k * 2 + b
                pe.wait_ge(hid_crossed, m + 1)
                x_part(b, 1, 0, True)
                x_part(b, 0, 1, True).then_inc(hid_ready, 1)

            def layer2(k, b, first=False):
                m = k * 2 + b
                pe.wait_ge(relu_done, m + 1)
                if not first:
                    pe.wait_ge(res_ready, m - 1)
                for j in range(4):
                    for c in range(2):
                        mm = nc.tensor.matmul(ps_y[b][:, j * D:(j + 1) * D], hid[b][:, c, j * P:(j + 1) * P], w_2[:, c, :], start=(c == 0), stop=(c == 1))
                mm.then_inc(y_ready, 1)

            gather(0, 0, True)
            gather(0, 1, True)
            layer1_start(0, 0)
            layer1_end(0, 0)
            for b in range(2):
                gather(1, b)
                layer1_start(b, 1 - b)
                layer2(0, b, True)
                layer1_end(b, 1 - b)
            with pe.Fori(2, HALF) as k:
                for b in range(2):
                    gather(k, b)
                    layer1_start(k - 1 + b, 1 - b)
                    layer2(k - 1, b)
                    layer1_end(k - 1 + b, 1 - b)
            layer1_start(HALF - 1, 1)
            layer2(HALF - 1, 0)
            layer1_end(HALF - 1, 1)
            layer2(HALF - 1, 1)


def kernel(x, src, dst, edge_attr_64, L0_gnn_W1, L0_gnn_b1, L0_gnn_W2, L0_gnn_b2):
    import numpy as np
    import concourse.bacc as bacc
    from concourse.bass_utils import run_bass_kernel_spmd

    def padded(a, rows, value):
        a = np.asarray(a)
        return np.concatenate([a, np.full((rows - a.shape[0],) + a.shape[1:], value, a.dtype)])

    x = padded(x, N_PAD, 0)
    arrays = {
        "x": x,
        "x_cols": np.ascontiguousarray(x.reshape(MACROS, 2, MACRO // 2, D).transpose(1, 3, 0, 2)).reshape(P, -1), "src": padded(src, E_PAD, N_PAD - 1), "dst": padded(dst, E_PAD, N_PAD - 1),
        "dst_next": padded(dst, E_PAD + 1, N_PAD - 1)[1:],
        "edge": padded(edge_attr_64, E_PAD, 0), "w1": np.asarray(L0_gnn_W1), "b1": np.asarray(L0_gnn_b1),
        "w2": np.asarray(L0_gnn_W2), "b2": np.asarray(L0_gnn_b2),
    }
    nc = bacc.Bacc("TRN2", target_bir_lowering=False, num_devices=1)
    args = [nc.dram_tensor(f"{n}_dram", a.shape, mybir.dt.from_np(a.dtype), kind="ExternalInput").ap() for n, a in arrays.items()]
    result = nc.dram_tensor("out_dram", (N_PAD, D), F32, kind="ExternalOutput").ap()
    gnn_kernel(nc, *args, result)
    r = run_bass_kernel_spmd(nc, [{f"{n}_dram": a for n, a in arrays.items()}], core_ids=[0])
    return r.results[0]["out_dram"][:N_NODES]
```

```python
import concourse.bass as bass
from concourse import mybir
from contextlib import ExitStack

ALU = mybir.AluOpType
ACT = mybir.ActivationFunctionType
F32 = mybir.dt.float32
F16 = mybir.dt.float16
I32 = mybir.dt.int32
AX_X = mybir.AxisListType.X

P = 128
D = 64
H = 256
N_NODES = 50000
N_EDGES = 25000
MACRO = 4 * P
MACROS = -(-N_NODES // MACRO)
N_PAD = MACROS * MACRO
BINS = N_PAD // P
ET = -(-N_EDGES // P)
E_PAD = ET * P
ROW = D + 2
TRASH = N_PAD
EPS = 1e-5
STEP = 14
PAIRS = STEP // 2
STEPS = ET // STEP
HALVES = [(0, 6), (6, STEP)]
BC = BINS // 4
PART = 3 * STEP
CUTS = [0] + [STEP + c for c in range(0, ET - STEP, PART)] + [ET]
PARTS = list(zip(CUTS[:-1], CUTS[1:]))
LOAD_PARTS = len(PARTS)
BAND = 32
BANDS = P // BAND
BAND_DMAS = 4
ROOM = [(0, 2, 1), (2, 6, 2), (6, 9, 3), (9, STEPS, BANDS)]
INIT_PARTS = 7
INIT_TILES = BINS // INIT_PARTS
FULL = 1 << 17


def gnn_kernel(nc, x, x_cols, src, dst, dst_next, edge, w1, b1, w2, b2, out):
    in_rows = nc.dram_tensor("in_rows", [N_PAD + P, ROW], F32)
    out_rows = nc.dram_tensor("out_rows", [N_PAD + P, ROW], F32)
    tables = [out_rows, in_rows]
    with ExitStack() as ctx:
        def sb(name, shape, dt=F32):
            return ctx.enter_context(nc.sbuf_tensor(name, shape, dt))

        def psum(name, shape, dt=F32):
            return ctx.enter_context(nc.psum_tensor(name, shape, dt))

        def sem(name):
            return ctx.enter_context(nc.semaphore(name))

        ident = sb("ident", [P, P])
        earlier = sb("earlier", [P, P])
        iota_row = sb("iota_row", [P, P])
        w_agg = sb("w_agg", [P, H])
        w_x = sb("w_x", [P, H])
        w_2 = sb("w_2", [P, 2, D])
        b_1 = sb("b_1", [P, 2])
        b_2 = sb("b_2", [P, D])
        eps = sb("eps", [P, 1])
        packed = sb("packed", [P, ET, ROW])
        ends_i = sb("ends_i", [P, 3, ET], I32)
        bins_i = sb("bins_i", [P, 4, ET], I32)
        ends = sb("ends", [P, 3, ET])
        bins = sb("bins", [P, ET])
        bin_base = sb("bin_base", [P, ET])
        sender_row = sb("sender_row", [P, ET])
        fall = sb("fall", [P, ET])
        bin_iota = sb("bin_iota", [P, BINS], F16)
        before = sb("before", [P, P], F16)
        not_before = sb("not_before", [P, P], F16)
        ones = sb("ones", [P, P], F16)
        bin_hot = [sb(f"bin_hot{i}", [P, BINS], F16) for i in range(STEP)]
        bin_junk = [sb(f"bin_junk{i}", [P, BINS]) for i in range(4)]
        rank = sb("rank", [P, STEP])
        over = sb("over", [P, STEP])
        placed = sb("placed", [P, STEP])
        slot = [sb(f"slot{i}", [P, 1], I32) for i in range(STEP)]
        staged_rows = [sb(f"staged_rows{i}", [P, ROW]) for i in range(STEP)]
        slots = sb("slots", [P, ET])
        tile_first = sb("tile_first", [P, BINS])
        tile_first_col = sb("tile_first_col", [BC, 4])
        row_length = sb("row_length", [P, 1])
        one_col = sb("one_col", [P, 1])
        next_below = sb("next_below", [P, BINS])
        row_hot = sb("row_hot", [P, BINS])
        smaller = sb("smaller", [BC, 4, ET])
        smaller_count = sb("smaller_count", [BC, 4])
        start_col = sb("start_col", [BC, 4])
        worst = sb("worst", [P, 3])
        worst_wide = sb("worst_wide", [P, P])
        first_edge = sb("first_edge", [1, BINS + 1])
        sizes = sb("sizes", [1, BINS])
        verdict = sb("verdict", [1, 3])
        unfit = sb("unfit", [1, 1], I32)
        window_start = sb("window_start", [1, BINS], I32)
        edge_part = [sb(f"edge_part{n}", [P, PART * D]) for n in range(2)]
        init = sb("init", [P, INIT_TILES, ROW])
        packed_rows = packed[:].rearrange("p t d -> p (t d)")
        zeros = sb("zeros", [MACROS, BAND * ROW])
        trash_row = sb("trash_row", [P, 1])
        idx_wide = [sb(f"idx_wide{j}", [P, P]) for j in range(2)]
        same = [sb(f"same{j}", [P, P]) for j in range(2)]
        junk = sb("junk", [P, P])
        dup = [sb(f"dup{j}", [P, 4]) for j in range(2)]
        row_index = [sb(f"row_index{j}", [P, 1], I32) for j in range(2)]
        stage = [sb(f"stage{j}", [P, ROW]) for j in range(2)]
        x_t = [sb(f"x_t{b}", [P, 4, D]) for b in range(2)]
        rows_t = [[sb(f"rows_t{j}{b}", [P, 4, ROW]) for b in range(2)] for j in range(2)]
        base = [sb(f"base{b}", [P, 4]) for b in range(2)]
        in_local = [sb(f"in_local{b}", [P, 4]) for b in range(2)]
        hot = [[sb(f"hot{j}{b}", [P, 4, P]) for b in range(2)] for j in range(2)]
        agg_T = [sb(f"agg_T{b}", [P, MACRO]) for b in range(2)]
        x_T = [sb(f"x_T{b}", [P, MACRO // 2]) for b in range(2)]
        hid = [sb(f"hid{b}", [P, 2, MACRO]) for b in range(2)]
        xb = [sb(f"xb{b}", [P, 4, D]) for b in range(2)]
        y_T = [sb(f"y_T{b}", [P, MACRO]) for b in range(2)]
        part_y = [sb(f"part_y{b}", [P, 4, D]) for b in range(2)]
        res = [sb(f"res{b}", [P, 4, D]) for b in range(2)]
        stats = [sb(f"stats{b}", [P, 4, 6]) for b in range(2)]
        both = [sb(f"both{b}", [P, 4, 2]) for b in range(2)]
        apart = [sb(f"apart{b}", [P, 4]) for b in range(2)]
        apart_sq = [sb(f"apart_sq{b}", [P, 4]) for b in range(2)]
        mean = [sb(f"mean{b}", [P, 4]) for b in range(2)]
        var_d = [sb(f"var_d{b}", [P, 4]) for b in range(2)]
        std = [sb(f"std{b}", [P, 4]) for b in range(2)]
        shift = [sb(f"shift{b}", [P, 4]) for b in range(2)]
        rstd = [sb(f"rstd{b}", [P, 4]) for b in range(2)]
        y_t = [sb(f"y_t{b}", [P, 4, D]) for b in range(2)]

        ps_agg = [psum(f"ps_agg{b}", [P, MACRO]) for b in range(2)]
        ps_hid = [psum(f"ps_hid{b}", [P, 2, MACRO]) for b in range(2)]
        ps_yT = psum("ps_yT", [P, MACRO])
        ps_y = psum("ps_y", [P, 4, P])
        ps_rank = [ps_yT, ps_y[:].rearrange("p j n -> p (j n)")]

        weights_in = sem("weights_in")
        ends_in = sem("ends_in")
        edges_in = [sem(f"edges_in{n}") for n in range(LOAD_PARTS)]
        zeros_made = sem("zeros_made")
        band_zeroed = [sem(f"band_zeroed{band}") for band in range(BANDS)]
        packed_ready = sem("packed_ready")
        edges_packed = sem("edges_packed")
        in_stored = sem("in_stored")
        prep_chain = sem("prep_chain")
        triangles = sem("triangles")
        hot_made = sem("hot_made")
        ranked = sem("ranked")
        pair_counted = sem("pair_counted")
        rank_read = sem("rank_read")
        slot_chain = sem("slot_chain")
        slots_made = sem("slots_made")
        rows_hot = sem("rows_hot")
        rows_picked = sem("rows_picked")
        start_chain = sem("start_chain")
        starts_turned = sem("starts_turned")
        staged = sem("staged")
        slot_made = sem("slot_made")
        scatters_begun = sem("scatters_begun")
        scattered = [sem(f"scattered{i}") for i in range(STEP)]
        worst_ready = sem("worst_ready")
        worst_turned = sem("worst_turned")
        verdict_chain = sem("verdict_chain")
        unfit_ready = sem("unfit_ready")
        tables_ready = sem("tables_ready")
        in_rows_new = sem("in_rows_new")
        consts = sem("consts")
        init_made = sem("init_made")
        table_settled = [sem("out_settled"), sem("in_settled")]
        idx_wide_ready = [sem(f"idx_wide_ready{j}") for j in range(2)]
        idx_row_ready = [sem(f"idx_row_ready{j}") for j in range(2)]
        same_ready = [sem(f"same_ready{j}") for j in range(2)]
        dup_chain = [sem(f"dup_chain{j}") for j in range(2)]
        additions_begun = sem("additions_begun")
        sums_ready = [sem(f"sums_ready{j}") for j in range(2)]
        stage_ready = [sem(f"stage_ready{j}") for j in range(2)]
        x_in = [sem(f"x_in{b}") for b in range(2)]
        out_rows_in = [sem(f"out_rows_in{b}") for b in range(2)]
        in_rows_in = [sem(f"in_rows_in{b}") for b in range(2)]
        local_ready = sem("local_ready")
        out_hot_ready = sem("out_hot_ready")
        agg_ready = sem("agg_ready")
        agg_copied = sem("agg_copied")
        hid_crossed = sem("hid_crossed")
        hid_begun = sem("hid_begun")
        hid_ready = sem("hid_ready")
        relu_done = sem("relu_done")
        yT_ready = sem("yT_ready")
        yT_copied = sem("yT_copied")
        y_ready = sem("y_ready")
        part_added = sem("part_added")
        xb_ready = sem("xb_ready")
        res_ready = sem("res_ready")
        stats_ready = sem("stats_ready")
        mv_chain = sem("mv_chain")
        mv_ready = sem("mv_ready")
        std_ready = sem("std_ready")
        rstd_ready = sem("rstd_ready")
        shift_ready = sem("shift_ready")
        y_done = sem("y_done")
        stored = [sem(f"stored{b}") for b in range(2)]

        INIT = (INIT_PARTS + 1) * 16
        HALF = MACROS // 2

        block = ctx.enter_context(nc.Block())

        @block.sync
        def _(sp):
            for k, e in enumerate((src, dst, dst_next)):
                sp.dma_start(ends_i[:, k, :], e.rearrange("(p t) -> p t", p=P)).then_inc(ends_in, 16)
            edge_parts = edge.rearrange("(p t) d -> p (t d)", p=P)

            def load_edges(n):
                lo, hi = PARTS[n]
                if n >= 2:
                    sp.wait_ge(edges_packed, n - 1)
                sp.dma_start(edge_part[n % 2][:, 0:(hi - lo) * D], edge_parts[:, lo * D:hi * D]).then_inc(edges_in[n], 16)

            load_edges(0)
            sp.wait_ge(band_zeroed[0], BAND_DMAS * 16)
            load_edges(1)
            sp.dma_start(w_agg[:], w1[0:P, :]).then_inc(weights_in, 16)
            for half in range(2):
                sp.dma_start(w_x[half * D:(half + 1) * D, :], w1[P:P + D, :]).then_inc(weights_in, 16)
            sp.dma_start(w_2[:], w2.rearrange("(c p) d -> p c d", p=P)).then_inc(weights_in, 16)
            with nc.allow_non_contiguous_dma(reason="256 values"):
                sp.dma_start(b_1[:], b1.rearrange("(c p) -> p c", p=P)).then_inc(weights_in, 16)
            sp.dma_start(b_2[:], b2.rearrange("(o d) -> o d", o=1).to_broadcast([P, D])).then_inc(weights_in, 16)

            sp.wait_ge(packed_ready, 2)
            in_parts = in_rows[0:E_PAD, :].rearrange("(p t) d -> p (t d)", p=P)
            for n, (lo, hi) in enumerate(PARTS):
                sp.wait_ge(edges_packed, n + 1)
                if n:
                    sp.wait_ge(scattered[0], (hi // STEP - 1) * 16)
                sp.dma_start(in_parts[:, lo * ROW:hi * ROW], packed_rows[:, lo * ROW:hi * ROW]).then_inc(in_stored, 16)
                if n + 2 < LOAD_PARTS:
                    load_edges(n + 2)

            sp.wait_ge(in_stored, LOAD_PARTS * 16)
            sp.wait_ge(unfit_ready, 1)
            with sp.If(sp.value_load(unfit[0:1, 0:1], min_val=0, max_val=1) > 0):
                sp.wait_ge(tables_ready, 1)
                sp.sem_inc(in_rows_new, 1)

            def read_starts(k, b):
                m = k * 2 + b
                return nc.values_load_multi_w_load_instructions(window_start[0:1, bass.ds(m * 4, 4)], engines=(mybir.EngineType.SP,), min_val=0, max_val=N_PAD - P)[1]

            def load_in_rows(b, starts):
                for j in range(4):
                    sp.dma_start(rows_t[1][b][:, j, :], in_rows[bass.ds(starts[j], P), :]).then_inc(in_rows_in[b], 16)

            def load_out_rows(k, b):
                m = k * 2 + b
                sp.dma_start(rows_t[0][b][:].rearrange("p j d -> p (j d)"), out_rows[bass.ds(m * MACRO, MACRO), :].rearrange("(p j) d -> p (j d)", p=P)).then_inc(out_rows_in[b], 16)

            def load_rows(k, b):
                m = k * 2 + b
                starts = read_starts(k, b)
                sp.wait_ge(agg_ready, m - 1)
                sp.wait_ge(out_hot_ready, m - 1)
                load_out_rows(k, b)
                load_in_rows(b, starts)

            for b in range(2):
                load_in_rows(b, read_starts(0, b))
            sp.wait_ge(tables_ready, 1)
            load_out_rows(0, 0)
            load_out_rows(0, 1)
            load_rows(1, 0)
            load_rows(1, 1)
            with sp.Fori(2, HALF) as k:
                for b in range(2):
                    load_rows(k, b)

        @block.gpsimd
        def _(pool):
            nc.gpsimd.memset(ident[:], 0.0).then_inc(init_made, 1)
            nc.gpsimd.memset(earlier[:], 1.0).then_inc(init_made, 1)
            nc.gpsimd.memset(before[:], 1.0).then_inc(init_made, 1)
            nc.gpsimd.memset(not_before[:], 1.0).then_inc(init_made, 1)
            nc.gpsimd.memset(ones[:], 1.0).then_inc(triangles, 1)
            nc.gpsimd.iota(tile_first[:], [[P, BINS]], base=0, channel_multiplier=0, allow_small_or_imprecise_dtypes=True).then_inc(triangles, 1)
            nc.gpsimd.iota(tile_first_col[:], [[BC * P, 4]], base=0, channel_multiplier=P, allow_small_or_imprecise_dtypes=True).then_inc(triangles, 1)
            nc.gpsimd.memset(row_length[:], float(ET)).then_inc(triangles, 1)
            nc.gpsimd.memset(one_col[:], 1.0).then_inc(triangles, 1)
            nc.gpsimd.iota(bin_iota[:], [[1, BINS]], base=0, channel_multiplier=0, allow_small_or_imprecise_dtypes=True).then_inc(triangles, 1)
            pool.wait_ge(init_made, 4)
            nc.gpsimd.affine_select(out=before[:], in_=before[:], compare_op=ALU.is_gt, fill=0.0, base=0, pattern=[[1, P]], channel_multiplier=-1).then_inc(triangles, 1)
            nc.gpsimd.affine_select(out=not_before[:], in_=not_before[:], compare_op=ALU.is_ge, fill=0.0, base=0, pattern=[[-1, P]], channel_multiplier=1).then_inc(triangles, 1)
            nc.gpsimd.affine_select(out=ident[:], in_=ident[:], compare_op=ALU.not_equal, fill=1.0, base=0, pattern=[[-1, P]], channel_multiplier=1).then_inc(consts, 1)
            nc.gpsimd.affine_select(out=earlier[:], in_=earlier[:], compare_op=ALU.is_gt, fill=0.0, base=0, pattern=[[-1, P]], channel_multiplier=1).then_inc(consts, 1)
            nc.gpsimd.memset(eps[:], EPS).then_inc(consts, 1)
            nc.gpsimd.memset(stage[0][:], 0.0).then_inc(consts, 1)
            nc.gpsimd.memset(stage[1][:], 0.0).then_inc(consts, 1)
            nc.gpsimd.iota(iota_row[:], [[1, P]], base=0, channel_multiplier=0, allow_small_or_imprecise_dtypes=True).then_inc(consts, 1)
            for b in range(2):
                nc.gpsimd.iota(base[b][:], [[P, 4]], base=b * MACRO, channel_multiplier=0, allow_small_or_imprecise_dtypes=True).then_inc(consts, 1)
            nc.gpsimd.iota(trash_row[:], [[0, 1]], base=TRASH, channel_multiplier=1, allow_small_or_imprecise_dtypes=True).then_inc(consts, 1)

            def scatter(u, i):
                t = u * STEP + i
                pool.wait_ge(staged, t + 1)
                pool.wait_ge(slot_made, t + 1)
                pool.sem_inc(scatters_begun, 1)
                nc.gpsimd.indirect_dma_start(
                    out=out_rows[:, :], out_offset=bass.IndirectOffsetOnAxis(ap=slot[i][:], axis=0),
                    in_=staged_rows[i][:], in_offset=None, bounds_check=N_PAD - 1, oob_is_err=False).then_inc(scattered[i], 16)

            for first, end, bands in ROOM:
                for band in range(bands):
                    pool.wait_ge(band_zeroed[band], BAND_DMAS * 16)
                with pool.Fori(first, end) as u:
                    for i in range(STEP):
                        scatter(u, i)
            for i in range(STEP):
                pool.wait_ge(scattered[i], 16 * STEPS)
            pool.wait_ge(in_stored, LOAD_PARTS * 16)

            def add_all():
                nc.gpsimd.memset(init[:], 0.0).then_inc(init_made, 1)
                pool.wait_ge(init_made, 5)
                nc.gpsimd.iota(init[:, :, D:D + 1], [[0, INIT_TILES]], base=0, channel_multiplier=1, allow_small_or_imprecise_dtypes=True).then_inc(init_made, 1)
                nc.gpsimd.iota(window_start[:], [[P, BINS]], base=0, channel_multiplier=0).then_inc(init_made, 1)
                for q in range(INIT_PARTS):
                    lo = q * INIT_TILES * P
                    if q:
                        for j in range(2):
                            pool.wait_ge(table_settled[j], 16 * q)
                    nc.gpsimd.iota(init[:, :, D + 1:D + 2], [[P, INIT_TILES]], base=lo, channel_multiplier=1, allow_small_or_imprecise_dtypes=True).then_inc(init_made, 1)
                    pool.wait_ge(init_made, 8 + q)
                    rows = slice(lo, lo + INIT_TILES * P)
                    pool.dma_start(tables[0][rows, :].rearrange("(m p j) d -> p m (j d)", p=P, j=4), init[:].rearrange("p (m j) d -> p m (j d)", j=4)).then_inc(table_settled[0], 16)
                    pool.dma_start(tables[1][rows, :].rearrange("(c p) d -> p c d", p=P), init[:]).then_inc(table_settled[1], 16)
                for j in range(2):
                    pool.dma_start(tables[j][TRASH:TRASH + P, :], init[:, 0, :]).then_inc(table_settled[j], 16)
                with pool.Fori(0, ET) as t:
                    for j in range(2):
                        pool.wait_ge(stage_ready[j], t + 1)
                        pool.wait_ge(dup_chain[j], t * 4 + 4)
                        pool.wait_ge(table_settled[j], t * 16 + INIT)
                        pool.sem_inc(additions_begun, 1)
                        nc.gpsimd.indirect_dma_start(
                            out=tables[j][:, :], out_offset=bass.IndirectOffsetOnAxis(ap=row_index[j][:], axis=0),
                            in_=stage[j][:], in_offset=None, compute_op=ALU.add).then_inc(table_settled[j], 16)
                for j in range(2):
                    pool.wait_ge(table_settled[j], INIT + 16 * ET)

            pool.wait_ge(unfit_ready, 1)
            with pool.If(pool.value_load(unfit[0:1, 0:1], min_val=0, max_val=1) > 0):
                add_all()
            pool.sem_inc(tables_ready, 1)

            pool.wait_ge(weights_in, 6 * 16)

            def step(k, b, first=False):
                m = k * 2 + b
                pool.wait_ge(x_in[b], k * 32 + 32)
                if not first:
                    pool.wait_ge(res_ready, m - 1)
                nc.gpsimd.tensor_tensor(xb[b][:], x_t[b][:], b_2[:].unsqueeze(1).to_broadcast([P, 4, D]), ALU.add).then_inc(xb_ready, 1)

            step(0, 0, True)
            step(0, 1, True)
            with pool.Fori(1, HALF) as k:
                for b in range(2):
                    step(k, b)

        @block.vector
        def _(dve):
            nc.vector.memset(zeros[:], 0.0).then_inc(zeros_made, 1)
            nc.vector.memset(first_edge[0:1, BINS:BINS + 1], float(E_PAD)).then_inc(verdict_chain, 1)
            dve.wait_ge(ends_in, 3 * 16)
            nc.vector.tensor_scalar(bins_i[:, 0, :], ends_i[:, 0, :], 7, None, ALU.logical_shift_right).then_inc(prep_chain, 1)
            nc.vector.tensor_scalar(bins_i[:, 1, :], ends_i[:, 0, :], P - 1, None, ALU.bitwise_and).then_inc(prep_chain, 1)
            nc.vector.tensor_scalar(bins_i[:, 2, :], ends_i[:, 0, :], -MACRO, None, ALU.bitwise_and).then_inc(prep_chain, 1)
            nc.vector.tensor_copy(ends[:], ends_i[:]).then_inc(prep_chain, 1)
            dve.wait_ge(prep_chain, 4)
            nc.vector.tensor_copy(bins[:], bins_i[:, 0, :]).then_inc(prep_chain, 1)
            nc.vector.tensor_scalar(bins_i[:, 3, :], bins_i[:, 0, :], 3, None, ALU.bitwise_and).then_inc(prep_chain, 1)
            nc.vector.tensor_copy(packed[:, :, D], bins_i[:, 1, :]).then_inc(packed_ready, 1)
            nc.vector.tensor_copy(packed[:, :, D + 1], ends[:, 1, :]).then_inc(packed_ready, 1)
            nc.vector.tensor_tensor(fall[:], ends[:, 1, :], ends[:, 2, :], ALU.subtract).then_inc(prep_chain, 1)
            dve.wait_ge(prep_chain, 7)
            nc.vector.tensor_tensor(bin_base[:], bins_i[:, 2, :], bins_i[:, 3, :], ALU.add).then_inc(prep_chain, 1)
            nc.vector.tensor_reduce(worst[:, 0:1], fall[:], AX_X, ALU.max).then_inc(prep_chain, 1)
            dve.wait_ge(prep_chain, 9)
            dve.wait_ge(triangles, 8)

            AHEAD = 3

            def bin_hots(u, q, first=False):
                if not first:
                    dve.wait_ge(pair_counted, (u - 1) * PAIRS + q + 1)
                for i in (2 * q, 2 * q + 1):
                    t = u * STEP + i
                    nc.vector.tensor_scalar(bin_hot[i][:], bin_iota[:], bins[:, bass.ds(t, 1)], None, ALU.is_equal).then_inc(hot_made, 1)

            def read_ranks(u, q, first=False):
                for i in (2 * q, 2 * q + 1):
                    t = u * STEP + i
                    dve.wait_ge(ranked, t + 1)
                    if not (first and i < 4):
                        dve.wait_ge(rank_read, t - 3)
                    if not first:
                        dve.wait_ge(slot_chain, (u - 1) * 4 + (2 if i < HALVES[0][1] else 4))
                    nc.vector.tensor_tensor_reduce(out=bin_junk[i % 4][:], in0=ps_rank[i % 2][:, 0:BINS], in1=bin_hot[i][:], scale=1.0, scalar=0.0, op0=ALU.mult, op1=ALU.add, accum_out=rank[:, i:i + 1]).then_inc(rank_read, 1)

            def place(u, q, bands, first=False):
                for half, (lo, hi) in enumerate(HALVES):
                    if hi != 2 * q + 2:
                        continue
                    cols = slice(lo, hi)
                    n = u * 2 + half
                    dve.wait_ge(rank_read, u * STEP + hi)
                    if not first:
                        dve.wait_ge(slots_made, n - 1)
                    nc.vector.tensor_scalar(over[:, cols], rank[:, cols], float(bands * BAND), float(FULL), ALU.is_ge, ALU.mult).then_inc(slot_chain, 1)
                    dve.wait_ge(slot_chain, n * 2 + 1)
                    nc.vector.scalar_tensor_tensor(out=placed[:, cols], in0=rank[:, cols], scalar=4.0, in1=over[:, cols], op0=ALU.mult, op1=ALU.add).then_inc(slot_chain, 1)
                    dve.wait_ge(slot_chain, n * 2 + 2)
                    nc.vector.tensor_tensor(slots[:, bass.ds(u * STEP + lo, hi - lo)], placed[:, cols], bin_base[:, bass.ds(u * STEP + lo, hi - lo)], ALU.add).then_inc(slots_made, 1)

            for q in range(AHEAD):
                bin_hots(0, q, True)

            for q in range(PAIRS):
                read_ranks(0, q, True)
                if q + AHEAD < PAIRS:
                    bin_hots(0, q + AHEAD, True)
                else:
                    bin_hots(1, q + AHEAD - PAIRS)
                place(0, q, ROOM[0][2], True)
            for first, end, bands in ROOM:
                with dve.Fori(max(first, 1), min(end, STEPS - 1)) as u:
                    for q in range(PAIRS):
                        read_ranks(u, q)
                        if q + AHEAD < PAIRS:
                            bin_hots(u, q + AHEAD)
                        else:
                            bin_hots(u + 1, q + AHEAD - PAIRS)
                        place(u, q, bands)
            for q in range(PAIRS):
                read_ranks(STEPS - 1, q)
                if q + AHEAD < PAIRS:
                    bin_hots(STEPS - 1, q + AHEAD)
                place(STEPS - 1, q, BANDS)

            nc.vector.tensor_scalar(next_below[:], tile_first[:], ends[:, 2, ET - 1:ET], None, ALU.is_gt).then_inc(rows_hot, 1)
            dve.wait_ge(rows_hot, 1)
            nc.vector.scalar_tensor_tensor(out=row_hot[:], in0=tile_first[:], scalar=ends[:, 1, 0:1], in1=next_below[:], op0=ALU.is_gt, op1=ALU.subtract).then_inc(rows_hot, 1)

            for c in range(4):
                dve.wait_ge(rows_picked, c + 1)
                nc.vector.tensor_scalar(smaller[:, c, :], ps_hid[c // 2][0:BC, c % 2, 0:ET], tile_first_col[:, c:c + 1], None, ALU.is_lt).then_inc(start_chain, 1)
            dve.wait_ge(start_chain, 4)
            nc.vector.tensor_reduce(smaller_count[:], smaller[:], AX_X, ALU.add).then_inc(start_chain, 1)
            dve.wait_ge(start_chain, 5)
            for c in range(4):
                bank = ps_hid[c // 2][0:BC, c % 2, :]
                nc.vector.scalar_tensor_tensor(out=start_col[:, c:c + 1], in0=smaller_count[:, c:c + 1], scalar=bank[:, ET:ET + 1], in1=bank[:, ET + 1:ET + 2], op0=ALU.mult, op1=ALU.add).then_inc(start_chain, 1)
            dve.wait_ge(starts_turned, 1)
            nc.vector.tensor_copy(first_edge[0:1, 0:BINS], ps_agg[0][0:1, 0:BINS]).then_inc(verdict_chain, 1)
            dve.wait_ge(verdict_chain, 2)
            nc.vector.tensor_tensor(sizes[:], first_edge[0:1, 1:BINS + 1], first_edge[0:1, 0:BINS], ALU.subtract).then_inc(verdict_chain, 1)
            nc.vector.tensor_scalar(window_start[:], first_edge[0:1, 0:BINS], float(E_PAD - P), None, ALU.min).then_inc(verdict_chain, 1)
            dve.wait_ge(verdict_chain, 4)
            nc.vector.tensor_reduce(verdict[:, 0:1], sizes[:], AX_X, ALU.max).then_inc(verdict_chain, 1)

            dve.wait_ge(slots_made, STEPS * 2)
            nc.vector.tensor_reduce(worst[:, 1:2], slots[:], AX_X, ALU.max).then_inc(verdict_chain, 1)
            dve.wait_ge(verdict_chain, 6)
            nc.vector.scalar_tensor_tensor(out=worst[:, 2:3], in0=worst[:, 1:2], scalar=float(1 - FULL), in1=worst[:, 0:1], op0=ALU.add, op1=ALU.max).then_inc(verdict_chain, 1)
            dve.wait_ge(verdict_chain, 7)
            nc.vector.tensor_copy(worst_wide[:], worst[:, 2:3].to_broadcast([P, P])).then_inc(worst_ready, 1)
            dve.wait_ge(worst_turned, 1)
            nc.vector.tensor_reduce(verdict[:, 1:2], ps_hid[0][0:1, 0, 0:P], AX_X, ALU.max).then_inc(verdict_chain, 1)
            dve.wait_ge(verdict_chain, 8)
            nc.vector.scalar_tensor_tensor(out=verdict[:, 2:3], in0=verdict[:, 0:1], scalar=float(-P), in1=verdict[:, 1:2], op0=ALU.add, op1=ALU.max).then_inc(verdict_chain, 1)
            dve.wait_ge(verdict_chain, 9)
            nc.vector.tensor_scalar(unfit[:], verdict[:, 2:3], 0.0, None, ALU.is_gt).then_inc(unfit_ready, 1)

            def add_all():
                dve.wait_ge(consts, 9)
                nc.vector.scalar_tensor_tensor(out=sender_row[:], in0=packed[:, :, D], scalar=4.0, in1=bin_base[:], op0=ALU.mult, op1=ALU.add).then_inc(verdict_chain, 1)
                dve.wait_ge(verdict_chain, 10)
                table_row = [sender_row[:], ends[:, 1, :]]
                with dve.Fori(0, ET) as t:
                    for j in range(2):
                        nc.vector.tensor_copy(idx_wide[j][:], table_row[j][:, bass.ds(t, 1)].to_broadcast([P, P])).then_inc(idx_wide_ready[j], 1)
                    for j in range(2):
                        dve.wait_ge(idx_row_ready[j], t + 1)
                        nc.vector.tensor_scalar(same[j][:], ps_hid[j][:, 0, 0:P], idx_wide[j][:, 0:1], None, ALU.is_equal).then_inc(same_ready[j], 1)
                        dve.wait_ge(same_ready[j], t + 1)
                        nc.vector.tensor_tensor_reduce(out=junk[:], in0=same[j][:], in1=earlier[:], scale=1.0, scalar=0.0, op0=ALU.mult, op1=ALU.add, accum_out=dup[j][:, 0:1]).then_inc(dup_chain[j], 1)
                        nc.vector.tensor_tensor(dup[j][:, 1:2], trash_row[:], idx_wide[j][:, 0:1], ALU.subtract).then_inc(dup_chain[j], 1)
                        dve.wait_ge(dup_chain[j], t * 4 + 2)
                        nc.vector.tensor_scalar(dup[j][:, 2:3], dup[j][:, 0:1], 1.0, dup[j][:, 1:2], ALU.min, ALU.mult).then_inc(dup_chain[j], 1)
                        dve.wait_ge(dup_chain[j], t * 4 + 3)
                        dve.wait_ge(table_settled[j], t * 16 + INIT)
                        nc.vector.tensor_tensor(row_index[j][:], dup[j][:, 2:3], idx_wide[j][:, 0:1], ALU.add).then_inc(dup_chain[j], 1)
                        dve.wait_ge(dup_chain[j], t * 4 + 4)

            dve.wait_ge(unfit_ready, 1)
            with dve.If(dve.value_load(unfit[0:1, 0:1], min_val=0, max_val=1) > 0):
                add_all()
            dve.wait_ge(consts, 9)

            def in_hots(k, b, first=False):
                m = k * 2 + b
                dve.wait_ge(in_rows_in[b], k * 64 + 64)
                if not first:
                    dve.wait_ge(agg_ready, m - 1)
                nc.vector.tensor_tensor(in_local[b][:], rows_t[1][b][:, :, D + 1], base[b][:], ALU.subtract).then_inc(local_ready, 1)
                dve.wait_ge(local_ready, m * 2 + 1)
                nc.vector.tensor_tensor(hot[1][b][:], iota_row[:].unsqueeze(1).to_broadcast([P, 4, P]), in_local[b][:].unsqueeze(2).to_broadcast([P, 4, P]), ALU.is_equal)
                nc.vector.tensor_scalar(base[b][:], base[b][:], float(2 * MACRO), None, ALU.add).then_inc(local_ready, 1)

            def out_hots(k, b):
                dve.wait_ge(out_rows_in[b], k * 16 + 16)
                nc.vector.tensor_tensor(hot[0][b][:], iota_row[:].unsqueeze(1).to_broadcast([P, 4, P]), rows_t[0][b][:, :, D].unsqueeze(2).to_broadcast([P, 4, P]), ALU.is_equal).then_inc(out_hot_ready, 1)

            def hots(k, b):
                in_hots(k, b)
                out_hots(k, b)

            def agg_copy(k, b):
                m = k * 2 + b
                dve.wait_ge(agg_ready, m + 1)
                nc.vector.tensor_copy(agg_T[b][:], ps_agg[b][:]).then_inc(agg_copied, 1)

            def norm(k, b, first=False):
                m = k * 2 + b
                dve.wait_ge(y_ready, m + 1)
                dve.wait_ge(xb_ready, m + 1)
                if not first:
                    dve.wait_ge(y_done, m - 1)
                nc.vector.tensor_tensor(part_y[b][:], ps_y[:, :, 0:D], xb[b][:], ALU.add).then_inc(part_added, 1)
                dve.wait_ge(part_added, m + 1)
                nc.vector.tensor_tensor(res[b][:], ps_y[:, :, D:P], part_y[b][:], ALU.add).then_inc(res_ready, 1)
                dve.wait_ge(res_ready, m + 1)
                for j in range(4):
                    last = nc.vector.bn_stats(stats[b][:, j, :], res[b][:, j, :])
                last.then_inc(stats_ready, 1)
                dve.wait_ge(stats_ready, m + 1)
                nc.vector.tensor_tensor(both[b][:], stats[b][:, :, 1:3], stats[b][:, :, 4:6], ALU.add).then_inc(mv_chain, 1)
                nc.vector.tensor_tensor(apart[b][:], stats[b][:, :, 1], stats[b][:, :, 4], ALU.subtract).then_inc(mv_chain, 1)
                dve.wait_ge(mv_chain, m * 4 + 2)
                nc.vector.scalar_tensor_tensor(out=apart_sq[b][:], in0=apart[b][:], scalar=D / 4.0, in1=apart[b][:], op0=ALU.mult, op1=ALU.mult).then_inc(mv_chain, 1)
                nc.vector.tensor_scalar(mean[b][:], both[b][:, :, 0], 0.5, None, ALU.mult).then_inc(mv_chain, 1)
                dve.wait_ge(mv_chain, m * 4 + 4)
                nc.vector.tensor_tensor(var_d[b][:], both[b][:, :, 1], apart_sq[b][:], ALU.add).then_inc(mv_ready, 1)

            def scales(k, b, first=False):
                m = k * 2 + b
                dve.wait_ge(std_ready, m + 1)
                if not first:
                    dve.wait_ge(y_done, m - 1)
                nc.vector.reciprocal(rstd[b][:], std[b][:]).then_inc(rstd_ready, 1)
                dve.wait_ge(rstd_ready, m + 1)
                nc.vector.scalar_tensor_tensor(out=shift[b][:], in0=mean[b][:], scalar=-1.0, in1=rstd[b][:], op0=ALU.mult, op1=ALU.mult).then_inc(shift_ready, 1)

            in_hots(0, 0, True)
            in_hots(0, 1, True)
            out_hots(0, 0)
            out_hots(0, 1)
            agg_copy(0, 0)
            agg_copy(0, 1)
            hots(1, 0)
            for b in range(2):
                agg_copy(1, b)
                if b:
                    scales(0, 0, True)
                hots(1 + b, 1 - b)
                norm(0, b, True)
            with dve.Fori(2, HALF - 1) as k:
                for b in range(2):
                    agg_copy(k, b)
                    scales(k - 2 + b, 1 - b)
                    hots(k + b, 1 - b)
                    norm(k - 1, b)
            agg_copy(HALF - 1, 0)
            scales(HALF - 3, 1)
            hots(HALF - 1, 1)
            norm(HALF - 2, 0)
            agg_copy(HALF - 1, 1)
            scales(HALF - 2, 0)
            norm(HALF - 2, 1)
            scales(HALF - 2, 1)
            norm(HALF - 1, 0)
            scales(HALF - 1, 0)
            norm(HALF - 1, 1)
            scales(HALF - 1, 1)

        @block.scalar
        def _(act):
            act.wait_ge(zeros_made, 1)
            slots_of = out_rows[0:N_PAD, :].rearrange("(m s) d -> m (s d)", s=MACRO)

            def clear(band):
                for q in range(BAND_DMAS):
                    piece = (band * BAND_DMAS + q) * BAND * ROW
                    act.dma_start(slots_of[:, piece:piece + BAND * ROW], zeros[:]).then_inc(band_zeroed[band], 16)

            clear(0)
            nc.scalar.preload_act_table(ACT.Sqrt)
            act.wait_ge(packed_ready, 2)

            def stage_rows(u, i, first=False):
                t = u * STEP + i
                if not first:
                    act.wait_ge(scattered[i], u * 16)
                nc.scalar.copy(staged_rows[i][:], packed[:, bass.ds(t, 1), :].rearrange("p o d -> p (o d)")).then_inc(staged, 1)
                act.wait_ge(slots_made, u * 2 + (1 if i < HALVES[0][1] else 2))
                nc.scalar.copy(slot[i][:], slots[:, bass.ds(t, 1)]).then_inc(slot_made, 1)

            for n, (lo, hi) in enumerate(PARTS):
                if 0 < n < BANDS:
                    clear(n)
                act.wait_ge(edges_in[n], 16)
                nc.scalar.copy(packed[:, lo:hi, 0:D], edge_part[n % 2][:, 0:(hi - lo) * D].rearrange("p (t d) -> p t d", d=D)).then_inc(edges_packed, 1)
                act.wait_ge(edges_packed, n + 1)
                if n == 0:
                    for i in range(STEP):
                        stage_rows(0, i, True)
                else:
                    with act.Fori(lo // STEP, hi // STEP) as u:
                        for i in range(STEP):
                            stage_rows(u, i)

            def add_all():
                with act.Fori(0, ET) as t:
                    for j in range(2):
                        act.wait_ge(sums_ready[j], t + 1)
                        act.wait_ge(table_settled[j], t * 16 + INIT)
                        nc.scalar.copy(stage[j][:, 0:D], ps_hid[j][:, 1, 0:D]).then_inc(stage_ready[j], 1)

            act.wait_ge(unfit_ready, 1)
            with act.If(act.value_load(unfit[0:1, 0:1], min_val=0, max_val=1) > 0):
                add_all()
            act.wait_ge(consts, 9)
            act.wait_ge(weights_in, 6 * 16)

            def load_x(k, b, first=False):
                m = k * 2 + b
                if not first:
                    act.wait_ge(hid_ready, m - 1)
                    act.wait_ge(xb_ready, m - 1)
                act.dma_start(x_T[b][:], x_cols[:, bass.ds(m * (MACRO // 2), MACRO // 2)]).then_inc(x_in[b], 16)
                act.dma_start(x_t[b][:].rearrange("p j d -> p (j d)"), x[bass.ds(m * MACRO, MACRO), :].rearrange("(p j) d -> p (j d)", p=P)).then_inc(x_in[b], 16)

            def relu(k, b):
                m = k * 2 + b
                act.wait_ge(hid_ready, m + 1)
                for c in range(2):
                    last = nc.scalar.activation(hid[b][:, c, :], ps_hid[b][:, c, :], ACT.Relu, bias=b_1[:, c:c + 1])
                last.then_inc(relu_done, 1)

            def stds(k, b):
                m = k * 2 + b
                act.wait_ge(mv_ready, m + 1)
                nc.scalar.activation(std[b][:], var_d[b][:], ACT.Sqrt, bias=eps[:], scale=1.0 / D).then_inc(std_ready, 1)

            def finish(k, b, first=False):
                m = k * 2 + b
                act.wait_ge(shift_ready, m + 1)
                if not first:
                    act.wait_ge(stored[b], k * 16)
                for j in range(4):
                    last = nc.scalar.activation(y_t[b][:, j, :], res[b][:, j, :], ACT.Identity, bias=shift[b][:, j:j + 1], scale=rstd[b][:, j:j + 1])
                last.then_inc(y_done, 1)

            def store(k, b):
                m = k * 2 + b
                act.wait_ge(y_done, m + 1)
                act.dma_start(out[bass.ds(m * MACRO, MACRO), :].rearrange("(p j) d -> p (j d)", p=P), y_t[b][:].rearrange("p j d -> p (j d)")).then_inc(stored[b], 16)

            def y_copy(k, b):
                m = k * 2 + b
                act.wait_ge(yT_ready, m + 1)
                nc.scalar.copy(y_T[b][:], ps_yT[:]).then_inc(yT_copied, 1)

            load_x(0, 0, True)
            load_x(0, 1, True)
            relu(0, 0)
            load_x(1, 0)
            for b in range(2):
                y_copy(0, b)
                relu(b, 1 - b)
                load_x(1 + b, 1 - b)
                stds(0, b)
            finish(0, 0, True)
            store(0, 0)
            def steady(k, b):
                y_copy(k - 1, b)
                if b:
                    finish(k - 1, 0)
                else:
                    finish(k - 2, 1)
                relu(k - 1 + b, 1 - b)
                if b:
                    store(k - 1, 0)
                else:
                    store(k - 2, 1)

            with act.Fori(2, HALF - 1) as k:
                for b in range(2):
                    steady(k, b)
                    load_x(k + b, 1 - b)
                    stds(k - 1, b)
            steady(HALF - 1, 0)
            load_x(HALF - 1, 1)
            stds(HALF - 2, 0)
            steady(HALF - 1, 1)
            stds(HALF - 2, 1)
            y_copy(HALF - 1, 0)
            finish(HALF - 2, 1)
            relu(HALF - 1, 1)
            store(HALF - 2, 1)
            stds(HALF - 1, 0)
            y_copy(HALF - 1, 1)
            finish(HALF - 1, 0)
            store(HALF - 1, 0)
            stds(HALF - 1, 1)
            finish(HALF - 1, 1)
            store(HALF - 1, 1)
            for b in range(2):
                act.wait_ge(stored[b], 16 * HALF)

        @block.tensor
        def _(pe):
            def count(bank, lhsT, rhs, start=False):
                return nc.tensor.matmul(bank, lhsT, rhs, start=start, stop=True, skip_group_check=True)

            def rank_pair(u, q, first=False):
                even, odd = 2 * q, 2 * q + 1
                t = u * STEP + even
                pe.wait_ge(hot_made, t + 2)
                count(ps_rank[0][:, 0:BINS], before[:], bin_hot[even][:], first).then_inc(ranked, 1)
                count(ps_rank[1][:, 0:BINS], ones[:], bin_hot[even][:], first)
                count(ps_rank[1][:, 0:BINS], before[:], bin_hot[odd][:]).then_inc(ranked, 1)
                pe.wait_ge(rank_read, t + 1)
                count(ps_rank[0][:, 0:BINS], not_before[:], bin_hot[even][:])
                count(ps_rank[0][:, 0:BINS], ones[:], bin_hot[odd][:])
                pe.wait_ge(rank_read, t + 2)
                count(ps_rank[1][:, 0:BINS], not_before[:], bin_hot[odd][:]).then_inc(pair_counted, 1)

            pe.wait_ge(triangles, 8)
            pe.wait_ge(consts, 9)
            for q in range(PAIRS):
                rank_pair(0, q, q == 0)
            with pe.Fori(1, STEPS) as u:
                for q in range(PAIRS):
                    rank_pair(u, q)
            pe.wait_ge(rows_hot, 2)
            for c in range(4):
                bank = ps_hid[c // 2][0:BC, c % 2, :]
                tiles = slice(c * BC, (c + 1) * BC)
                nc.tensor.matmul(bank[:, 0:ET], row_hot[:, tiles], ends[:, 1, :], start=True, stop=True)
                nc.tensor.matmul(bank[:, ET:ET + 1], row_hot[:, tiles], one_col[:], start=True, stop=True)
                nc.tensor.matmul(bank[:, ET + 1:ET + 2], next_below[:, tiles], row_length[:], start=True, stop=True).then_inc(rows_picked, 1)
            pe.wait_ge(start_chain, 9)
            for c in range(4):
                last = nc.tensor.matmul(ps_agg[0][0:1, c * BC:(c + 1) * BC], start_col[:, c:c + 1], ident[0:BC, 0:BC], start=True, stop=True)
            last.then_inc(starts_turned, 1)
            pe.wait_ge(worst_ready, 1)
            nc.tensor.transpose(ps_hid[0][:, 0, 0:P], worst_wide[:], ident[:]).then_inc(worst_turned, 1)

            def add_all():
                pe.wait_ge(edges_packed, LOAD_PARTS)
                with pe.Fori(0, ET) as t:
                    for j in range(2):
                        pe.wait_ge(idx_wide_ready[j], t + 1)
                        nc.tensor.transpose(ps_hid[j][:, 0, 0:P], idx_wide[j][:], ident[:]).then_inc(idx_row_ready[j], 1)
                    for j in range(2):
                        pe.wait_ge(same_ready[j], t + 1)
                        nc.tensor.matmul(ps_hid[j][:, 1, 0:D], same[j][:], packed[:, bass.ds(t, 1), 0:D].rearrange("p o d -> p (o d)"), start=True, stop=True).then_inc(sums_ready[j], 1)
                    for j in range(2):
                        pe.wait_ge(stage_ready[j], t + 1)

            pe.wait_ge(unfit_ready, 1)
            with pe.If(pe.value_load(unfit[0:1, 0:1], min_val=0, max_val=1) > 0):
                add_all()
            pe.wait_ge(weights_in, 6 * 16)

            def gather(k, b, first=False):
                m = k * 2 + b
                pe.wait_ge(out_hot_ready, m + 1)
                if not first:
                    pe.wait_ge(agg_copied, m - 1)
                for j in range(4):
                    for side in range(2):
                        half = slice(D, P) if side == 0 else slice(0, D)
                        mm = nc.tensor.matmul(ps_agg[b][half, j * P:(j + 1) * P], rows_t[side][b][:, j, 0:D], hot[side][b][:, j, :], start=True, stop=True)
                mm.then_inc(agg_ready, 1)

            def x_part(b, c, half, start):
                rows = slice(half * D, (half + 1) * D)
                tiles = ps_hid[b][:, c, half * (MACRO // 2):(half + 1) * (MACRO // 2)]
                return nc.tensor.matmul(tiles, w_x[rows, c * P:(c + 1) * P], x_T[b][rows], start=start, stop=True, skip_group_check=True)

            def layer1_x(k, b):
                m = k * 2 + b
                pe.wait_ge(x_in[b], k * 32 + 32)
                x_part(b, 0, 0, True)
                x_part(b, 1, 1, True).then_inc(hid_crossed, 1)

            def layer1_x_crossed(k, b):
                m = k * 2 + b
                pe.wait_ge(hid_crossed, m + 1)
                x_part(b, 1, 0, False)
                x_part(b, 0, 1, False).then_inc(hid_begun, 1)

            def layer1_agg(k, b):
                m = k * 2 + b
                pe.wait_ge(agg_copied, m + 1)
                pe.wait_ge(hid_begun, m + 1)
                for c in range(2):
                    mm = nc.tensor.matmul(ps_hid[b][:, c, :], w_agg[:, c * P:(c + 1) * P], agg_T[b][:], start=False, stop=True, skip_group_check=True)
                mm.then_inc(hid_ready, 1)

            def layer2(k, b, first=False):
                m = k * 2 + b
                pe.wait_ge(relu_done, m + 1)
                if not first:
                    pe.wait_ge(yT_copied, m)
                for c in range(2):
                    mm = nc.tensor.matmul(ps_yT[c * D:(c + 1) * D, :], w_2[:, c, :], hid[b][:, c, :], start=True, stop=True)
                mm.then_inc(yT_ready, 1)

            def turn_y(k, b, first=False):
                m = k * 2 + b
                pe.wait_ge(yT_copied, m + 1)
                if not first:
                    pe.wait_ge(res_ready, m)
                by_four = y_T[b][:].rearrange("p (n j) -> p n j", j=4)
                for j in range(4):
                    mm = nc.tensor.transpose(ps_y[:, j, :], by_four[:, :, j], ident[:])
                mm.then_inc(y_ready, 1)

            for b in range(2):
                layer1_x(0, b)
                layer1_x_crossed(0, b)
            gather(0, 0, True)
            gather(0, 1, True)
            layer1_agg(0, 0)
            gather(1, 0)
            layer2(0, 0, True)
            turn_y(0, 0, True)
            layer1_agg(0, 1)
            gather(1, 1)
            layer1_x(1, 0)
            layer2(0, 1)
            layer1_x_crossed(1, 0)
            turn_y(0, 1)
            layer1_agg(1, 0)
            with pe.Fori(2, HALF) as k:
                for b in range(2):
                    gather(k, b)
                    layer1_x(k - 1 + b, 1 - b)
                    layer2(k - 1, b)
                    layer1_x_crossed(k - 1 + b, 1 - b)
                    turn_y(k - 1, b)
                    layer1_agg(k - 1 + b, 1 - b)
            layer1_x(HALF - 1, 1)
            layer2(HALF - 1, 0)
            layer1_x_crossed(HALF - 1, 1)
            turn_y(HALF - 1, 0)
            layer1_agg(HALF - 1, 1)
            layer2(HALF - 1, 1)
            turn_y(HALF - 1, 1)


def kernel(x, src, dst, edge_attr_64, L0_gnn_W1, L0_gnn_b1, L0_gnn_W2, L0_gnn_b2):
    import numpy as np
    import concourse.bacc as bacc
    from concourse.bass_utils import run_bass_kernel_spmd

    def padded(a, rows, value):
        a = np.asarray(a)
        return np.concatenate([a, np.full((rows - a.shape[0],) + a.shape[1:], value, a.dtype)])

    x = padded(x, N_PAD, 0)
    arrays = {
        "x": x,
        "x_cols": np.ascontiguousarray(x.reshape(MACROS, 2, MACRO // 2, D).transpose(1, 3, 0, 2)).reshape(P, -1),
        "src": padded(src, E_PAD, N_PAD - 1), "dst": padded(dst, E_PAD, N_PAD - 1),
        "dst_next": padded(dst, E_PAD + 1, N_PAD - 1)[1:],
        "edge": padded(edge_attr_64, E_PAD, 0), "w1": np.asarray(L0_gnn_W1), "b1": np.asarray(L0_gnn_b1),
        "w2": np.asarray(L0_gnn_W2), "b2": np.asarray(L0_gnn_b2),
    }
    nc = bacc.Bacc("TRN2", target_bir_lowering=False, num_devices=1)
    args = [nc.dram_tensor(f"{n}_dram", a.shape, mybir.dt.from_np(a.dtype), kind="ExternalInput").ap() for n, a in arrays.items()]
    result = nc.dram_tensor("out_dram", (N_PAD, D), F32, kind="ExternalOutput").ap()
    gnn_kernel(nc, *args, result)
    r = run_bass_kernel_spmd(nc, [{f"{n}_dram": a for n, a in arrays.items()}], core_ids=[0])
    return r.results[0]["out_dram"][:N_NODES]
```
